# Optimizing a Trainium2 kernel written in Bass

```python
import numpy as np
import jax
import jax.numpy as jnp

def _softmax(x, axis=-1):
    return jax.nn.softmax(x, axis=axis)

def _gelu(x):
    return jax.nn.gelu(x, approximate=True)

def _silu(x):
    return jax.nn.silu(x)

def _sigmoid(x):
    return jax.nn.sigmoid(x)

def _layernorm(x, axis=-1, eps=1e-05):
    m = jnp.mean(x, axis=axis, keepdims=True)
    v = jnp.var(x, axis=axis, keepdims=True)
    return (x - m) / jnp.sqrt(v + eps)

def _scatter_add(tgt, idx, src, axis=0):
    return tgt.at[idx].add(src)

def _segment_sum(src, seg, n):
    return jax.ops.segment_sum(src, seg, n)
kernel_name = 'mk_perceiver_d1_seqx_r8_d2a0ea'

def setup_inputs(seed: int=0):
    np.random.seed(seed)
    _w = jnp.asarray

    def _rec_inputs():
        import jax
        import jax.numpy as jnp
        _rk = jax.random.key(seed)
        x = -0.0003929 + 0.9999 * jax.random.normal(jax.random.fold_in(_rk, 1), (128, 32, 128), jnp.float32)
        _lenS = 32 - jax.random.randint(jax.random.fold_in(_rk, 7), (128,), 0, max(1, 32 // 4) + 1, jnp.int32)
        _lenS2 = 257 - jax.random.randint(jax.random.fold_in(_rk, 8), (128,), 0, max(1, 257 // 4) + 1, jnp.int32)
        _ctx_768P = jax.random.normal(jax.random.fold_in(_rk, 11), (128, 16, 96), jnp.float32)
        _ctx_768c = jax.random.dirichlet(jax.random.fold_in(_rk, 511), 0.3 * jnp.ones((16,), jnp.float32), (128, 257))
        _ctx_768t = jnp.einsum('bsk,bkd->bsd', _ctx_768c, _ctx_768P)
        _ctx_768t = _ctx_768t * jax.lax.rsqrt(jnp.mean(jnp.square(_ctx_768t)) + 1e-12) * 0.953939
        ctx_768 = -0.00055796 + 0.999787 * (_ctx_768t + 0.3 * jax.random.normal(jax.random.fold_in(_rk, 611), (128, 257, 96), jnp.float32))
        return (x, ctx_768)
    x, ctx_768 = _rec_inputs()

    def _L0_xattn_setup():
        import jax, jax.numpy as jnp
        import numpy as np
        HEADS = 16
        DIM_HEAD = 64
        SCALE = DIM_HEAD ** (-0.5)
        key = jax.random.key(seed)
        ks = jax.random.split(key, 6)
        B, N, C = (4, 512, 128)
        M, Cc = (64, 96)
        inner = HEADS * DIM_HEAD
        s = lambda d: d ** (-0.5)
        return {'x': jax.random.normal(ks[0], (B, N, C), jnp.float32), 'context': jax.random.normal(ks[1], (B, M, Cc), jnp.float32), 'Wq': jax.random.normal(ks[2], (C, inner), jnp.float32) * s(C), 'Wk': jax.random.normal(ks[3], (Cc, inner), jnp.float32) * s(Cc), 'Wv': jax.random.normal(ks[4], (Cc, inner), jnp.float32) * s(Cc), 'Wo': jax.random.normal(ks[5], (inner, C), jnp.float32) * s(inner), 'bo': jnp.zeros((C,), jnp.float32)}
    _L0_xattn_all = _L0_xattn_setup()
    _L0_xattn_in = {k: v for k, v in _L0_xattn_all.items() if k in ('Wq', 'Wk', 'Wv', 'Wo', 'bo')}
    del _L0_xattn_all

    def _L0_attn_setup():
        import jax, jax.numpy as jnp
        import numpy as np
        B, T, C, H = (4, 256, 128, 16)
        D = C // H

        def _wkv_parallel(k, v, exp_w, exp_u):
            Tn = k.shape[1]
            exp_k = jnp.exp(k)
            exp_ek_v = exp_k * v
            t_idx = jnp.arange(Tn, dtype=k.dtype)
            log_alpha = jnp.log(exp_w)
            alpha_pow = jnp.exp(t_idx[None, :, None, None] * log_alpha)
            alpha_next_pow = alpha_pow * exp_w
            f_a = exp_ek_v / alpha_next_pow
            f_b = exp_k.sum(-1, keepdims=True) / alpha_next_pow
            cs_a = jnp.cumsum(f_a, axis=1)
            cs_b = jnp.cumsum(f_b, axis=1)
            zero_a = jnp.zeros_like(cs_a[:, :1])
            zero_b = jnp.zeros_like(cs_b[:, :1])
            excl_a = jnp.concatenate([zero_a, cs_a[:, :-1]], axis=1)
            excl_b = jnp.concatenate([zero_b, cs_b[:, :-1]], axis=1)
            state_a = jnp.nan_to_num(alpha_pow * excl_a, nan=0.0, posinf=0.0)
            state_b = jnp.nan_to_num(alpha_pow * excl_b, nan=0.0, posinf=0.0)
            exp_u_k = exp_u * exp_k
            num = state_a + exp_u_k * v
            den = jnp.maximum(state_b + exp_u_k.sum(-1, keepdims=True), 1e-06)
            return num / den
        key = jax.random.key(seed)
        ks = jax.random.split(key, 10)
        s = 1.0 / np.sqrt(C)
        return {'x': jax.random.normal(ks[0], (B, T, C), jnp.float32), 'mix_k': jax.random.uniform(ks[1], (1, 1, C), jnp.float32), 'mix_v': jax.random.uniform(ks[2], (1, 1, C), jnp.float32), 'mix_r': jax.random.uniform(ks[3], (1, 1, C), jnp.float32), 'W_key': jax.random.normal(ks[4], (C, C), jnp.float32) * s, 'W_value': jax.random.normal(ks[5], (C, C), jnp.float32) * s, 'W_receptance': jax.random.normal(ks[6], (C, C), jnp.float32) * s, 'W_output': jax.random.normal(ks[7], (C, C), jnp.float32) * s, 'time_decay': jax.random.normal(ks[8], (H,), jnp.float32) - 5.0, 'time_first': jax.random.normal(ks[9], (H,), jnp.float32)}
    _L0_attn_all = _L0_attn_setup()
    _L0_attn_in = {k: v for k, v in _L0_attn_all.items() if k in ('mix_k', 'mix_v', 'mix_r', 'W_key', 'W_value', 'W_receptance', 'W_output', 'time_decay', 'time_first')}
    del _L0_attn_all

    def _L0_ffn_setup():
        import jax, jax.numpy as jnp
        import numpy as np
        D_MODEL, D_FF, N_EXP = (128, 512, 8)
        key = jax.random.key(seed)
        ks = jax.random.split(key, 8)
        s = lambda fan_in: 1.0 / np.sqrt(fan_in)
        x = jax.random.normal(ks[0], (4, 256, D_MODEL), dtype=jnp.float32)
        Wr = jax.random.uniform(ks[1], (N_EXP, D_MODEL), jnp.float32, -s(D_MODEL), s(D_MODEL))
        br = jax.random.uniform(ks[2], (N_EXP,), jnp.float32, -s(D_MODEL), s(D_MODEL))
        W1 = jax.random.uniform(ks[3], (N_EXP, D_FF, D_MODEL), jnp.float32, -s(D_MODEL), s(D_MODEL))
        b1 = jax.random.uniform(ks[4], (N_EXP, D_FF), jnp.float32, -s(D_MODEL), s(D_MODEL))
        W2 = jax.random.uniform(ks[5], (N_EXP, D_MODEL, D_FF), jnp.float32, -s(D_FF), s(D_FF))
        b2 = jax.random.uniform(ks[6], (N_EXP, D_MODEL), jnp.float32, -s(D_FF), s(D_FF))
        return {'x': x, 'Wr': Wr, 'br': br, 'W1': W1, 'b1': b1, 'W2': W2, 'b2': b2}
    _L0_ffn_all = _L0_ffn_setup()
    _L0_ffn_in = {k: v for k, v in _L0_ffn_all.items() if k in ('Wr', 'br', 'W1', 'b1', 'W2', 'b2')}
    del _L0_ffn_all
    return {'x': x, 'ctx_768': ctx_768, 'L0_xattn_Wq': _L0_xattn_in['Wq'], 'L0_xattn_Wk': _L0_xattn_in['Wk'], 'L0_xattn_Wv': _L0_xattn_in['Wv'], 'L0_xattn_Wo': _L0_xattn_in['Wo'], 'L0_xattn_bo': _L0_xattn_in['bo'], 'L0_attn_mix_k': _L0_attn_in['mix_k'], 'L0_attn_mix_v': _L0_attn_in['mix_v'], 'L0_attn_mix_r': _L0_attn_in['mix_r'], 'L0_attn_W_key': _L0_attn_in['W_key'], 'L0_attn_W_value': _L0_attn_in['W_value'], 'L0_attn_W_receptance': _L0_attn_in['W_receptance'], 'L0_attn_W_output': _L0_attn_in['W_output'], 'L0_attn_time_decay': _L0_attn_in['time_decay'], 'L0_attn_time_first': _L0_attn_in['time_first'], 'L0_ffn_Wr': _L0_ffn_in['Wr'], 'L0_ffn_br': _L0_ffn_in['br'], 'L0_ffn_W1': _L0_ffn_in['W1'], 'L0_ffn_b1': _L0_ffn_in['b1'], 'L0_ffn_W2': _L0_ffn_in['W2'], 'L0_ffn_b2': _L0_ffn_in['b2']}

def reference(x, ctx_768, L0_xattn_Wq, L0_xattn_Wk, L0_xattn_Wv, L0_xattn_Wo, L0_xattn_bo, L0_attn_mix_k, L0_attn_mix_v, L0_attn_mix_r, L0_attn_W_key, L0_attn_W_value, L0_attn_W_receptance, L0_attn_W_output, L0_attn_time_decay, L0_attn_time_first, L0_ffn_Wr, L0_ffn_br, L0_ffn_W1, L0_ffn_b1, L0_ffn_W2, L0_ffn_b2):
    import jax
    import jax.numpy as jnp

    def _L0_xattn_ref(x, context, Wq, Wk, Wv, Wo, bo):
        import jax, jax.numpy as jnp
        import numpy as np
        HEADS = 16
        DIM_HEAD = 64
        SCALE = DIM_HEAD ** (-0.5)
        B, N, _ = x.shape
        M = context.shape[1]
        q = (x @ Wq).reshape(B, N, HEADS, DIM_HEAD).transpose(0, 2, 1, 3)
        k = (context @ Wk).reshape(B, M, HEADS, DIM_HEAD).transpose(0, 2, 1, 3)
        v = (context @ Wv).reshape(B, M, HEADS, DIM_HEAD).transpose(0, 2, 1, 3)
        dots = jnp.einsum('bhnd,bhmd->bhnm', q, k) * SCALE
        attn = jax.nn.softmax(dots, axis=-1)
        out = jnp.einsum('bhnm,bhmd->bhnd', attn, v)
        out = out.transpose(0, 2, 1, 3).reshape(B, N, HEADS * DIM_HEAD)
        return out @ Wo + bo

    def _L0_attn_ref(x, mix_k, mix_v, mix_r, W_key, W_value, W_receptance, W_output, time_decay, time_first):
        import jax, jax.numpy as jnp
        import numpy as np
        B, T, C, H = (4, 256, 128, 16)
        D = C // H

        def _wkv_parallel(k, v, exp_w, exp_u):
            Tn = k.shape[1]
            exp_k = jnp.exp(k)
            exp_ek_v = exp_k * v
            t_idx = jnp.arange(Tn, dtype=k.dtype)
            log_alpha = jnp.log(exp_w)
            alpha_pow = jnp.exp(t_idx[None, :, None, None] * log_alpha)
            alpha_next_pow = alpha_pow * exp_w
            f_a = exp_ek_v / alpha_next_pow
            f_b = exp_k.sum(-1, keepdims=True) / alpha_next_pow
            cs_a = jnp.cumsum(f_a, axis=1)
            cs_b = jnp.cumsum(f_b, axis=1)
            zero_a = jnp.zeros_like(cs_a[:, :1])
            zero_b = jnp.zeros_like(cs_b[:, :1])
            excl_a = jnp.concatenate([zero_a, cs_a[:, :-1]], axis=1)
            excl_b = jnp.concatenate([zero_b, cs_b[:, :-1]], axis=1)
            state_a = jnp.nan_to_num(alpha_pow * excl_a, nan=0.0, posinf=0.0)
            state_b = jnp.nan_to_num(alpha_pow * excl_b, nan=0.0, posinf=0.0)
            exp_u_k = exp_u * exp_k
            num = state_a + exp_u_k * v
            den = jnp.maximum(state_b + exp_u_k.sum(-1, keepdims=True), 1e-06)
            return num / den
        Bn, Tn, Cn = x.shape
        x_prev = jnp.pad(x, ((0, 0), (1, 0), (0, 0)))[:, :-1]
        k = (x * mix_k + x_prev * (1.0 - mix_k)) @ W_key.T
        v = (x * mix_v + x_prev * (1.0 - mix_v)) @ W_value.T
        r = jax.nn.sigmoid((x * mix_r + x_prev * (1.0 - mix_r)) @ W_receptance.T)
        k4 = k.reshape(Bn, Tn, H, D)
        v4 = v.reshape(Bn, Tn, H, D)
        exp_w = jnp.exp(-jnp.exp(time_decay)).reshape(1, 1, H, 1)
        exp_u = jnp.exp(time_first).reshape(1, 1, H, 1)
        wkv = _wkv_parallel(k4, v4, exp_w, exp_u).reshape(Bn, Tn, Cn)
        return r * wkv @ W_output.T

    def _L0_ffn_ref(x, Wr, br, W1, b1, W2, b2):
        import jax, jax.numpy as jnp
        import numpy as np
        D_MODEL, D_FF, N_EXP = (128, 512, 8)
        B, S, D = x.shape
        xf = x.reshape(-1, D)
        logits = xf @ Wr.T + br
        expert_idx = jnp.argmax(logits, axis=-1)
        h = jax.nn.relu(jnp.einsum('td,efd->etf', xf, W1) + b1[:, None, :])
        y = jnp.einsum('etf,edf->etd', h, W2) + b2[:, None, :]
        out = y[expert_idx, jnp.arange(xf.shape[0])]
        return out.reshape(B, S, D)
    x = x + _L0_xattn_ref(_layernorm(x, axis=-1), ctx_768, L0_xattn_Wq, L0_xattn_Wk, L0_xattn_Wv, L0_xattn_Wo, L0_xattn_bo)
    x = x + _L0_attn_ref(_layernorm(x, axis=-1), L0_attn_mix_k, L0_attn_mix_v, L0_attn_mix_r, L0_attn_W_key, L0_attn_W_value, L0_attn_W_receptance, L0_attn_W_output, L0_attn_time_decay, L0_attn_time_first)
    x = x + _L0_ffn_ref(_layernorm(x, axis=-1), L0_ffn_Wr, L0_ffn_br, L0_ffn_W1, L0_ffn_b1, L0_ffn_W2, L0_ffn_b2)
    return x

_drawn_inputs = setup_inputs


def setup_inputs(seed=0):
    import zlib

    import numpy as np

    out = dict(_drawn_inputs(seed))
    spreads = {'L0_xattn_bo': (0.0, 0.1)}
    factors = {'L0_attn_mix_k': 3.364,
     'L0_attn_mix_v': 2.957,
     'L0_attn_mix_r': 3.138,
     'L0_attn_time_decay': 7.86,
     'L0_attn_time_first': 2.749,
     'L0_ffn_b1': 3.193}
    for name, (base, spread) in spreads.items():
        noise = np.random.default_rng([zlib.crc32(name.encode()), seed]).standard_normal(out[name].shape)
        drawn = base * np.exp(spread * noise) if base else spread * noise
        out[name] = jnp.asarray(drawn.astype(out[name].dtype))
    for name, factor in factors.items():
        out[name] = (out[name] * factor).astype(out[name].dtype)
    return out
```

```python
from contextlib import ExitStack

import concourse.bass as bass
from concourse import mybir

ALU = mybir.AluOpType
ACT = mybir.ActivationFunctionType
AX = mybir.AxisListType
F32 = mybir.dt.float32
F16 = mybir.dt.float16

P = 128
EPS = 1e-5
FMAX = 3.4028234663852886e38


def wait(eng, sem, value):
    if isinstance(value, int) and value <= 0:
        return
    eng.wait_ge(sem, value)


class Chain:

    def __init__(self, eng, sem):
        self.eng, self.sem, self.base, self.count = eng, sem, 0, 0

    def at(self, base):
        self.base, self.count = base, 0

    def link(self, ins):
        self.count += 1
        ins.then_inc(self.sem, 1)
        self.eng.wait_ge(self.sem, self.base + self.count)

    def mark(self, ins):
        self.count += 1
        ins.then_inc(self.sem, 1)


def perceiver_layer_kernel(nc, x, ctx, Wq, Wk, Wv, Wo, bo, mix_k, mix_v, mix_r, W_key, W_value,
                           W_rec, W_out, decay, first, Wr, br, W1, b1, W2, b2, out):
    B, N, C = x.shape
    _, M, CC = ctx.shape
    HD = Wq.shape[1]
    H = 16
    D = HD // H
    SCALE = float(D) ** -0.5
    TOK = B * N
    G = TOK // P
    GB = P // N
    QT = H * N // P
    Q = H * N
    MC = M // P
    LAST = M - 1
    assert M == MC * P + 1 and Q == 512
    NP2 = 2
    CH = 8
    CT = G // CH
    SEQ = CT * GB
    T = CT * P
    E = Wr.shape[0]
    FF = W1.shape[1]
    FC = FF // P
    HS = C // H
    R3 = 3
    LR = R3 * QT

    top = ExitStack()

    def sb(name, shape, dt=F32):
        return top.enter_context(nc.sbuf_tensor(name, shape, dt))

    def sem(name):
        return top.enter_context(nc.semaphore(name))

    with top:
        bank = [top.enter_context(nc.psum_tensor(f"bank{i}", [P, 512], F32)) for i in range(8)]

        X = sb("X", [P, G, C])
        identf = sb("identf", [P, P])
        one = sb("one", [P, 1])
        ident = sb("ident", [P, P], F16)
        stats = sb("stats", [P, G, 6])
        mean = sb("mean", [P, G])
        std = sb("std", [P, G])
        rst = sb("rst", [P, G])
        tmpv = sb("tmpv", [P, G])
        varp = sb("varp", [P, G])
        xn = sb("xn", [P, 2, CT, C])

        s_id = sem("s_id")
        s_const = sem("s_const")
        s_x = sem("s_x")
        s_stat = sem("s_stat")
        s_var = sem("s_var")
        s_std = sem("s_std")
        s_ln = sem("s_ln")
        s_out = sem("s_out")

        s_w = sem("s_w")
        s_wT = sem("s_wT")
        s_wTc = sem("s_wTc")
        s_ab = sem("s_ab")
        s_abh = sem("s_abh")
        s_abl = sem("s_abl")
        s_xn1 = sem("s_xn1")
        s_x1T = sem("s_x1T")
        s_x1h = sem("s_x1h")
        s_x1l = sem("s_x1l")
        s_bo = sem("s_bo")
        s_raw0 = sem("s_raw0")
        s_p1end = sem("s_p1end")
        s_ctx = [sem(f"s_ctx{i}") for i in range(NP2)]
        s_chi = sem("s_chi")
        s_clo = sem("s_clo")
        s_h12 = sem("s_h12")
        s_g12 = sem("s_g12")
        s_c3 = sem("s_c3")
        s_z = sem("s_z")
        s_ctxT = sem("s_ctxT")
        s_cT = sem("s_cT")
        s_q = sem("s_q")
        s_qh = sem("s_qh")
        s_ql = sem("s_ql")
        s_S = sem("s_S")
        s_nmax = sem("s_nmax")
        s_exp = sem("s_exp")
        s_rs = sem("s_rs")
        s_pn = sem("s_pn")
        s_ehi = sem("s_ehi")
        s_elo = sem("s_elo")
        s_left = sem("s_left")
        s_L12 = sem("s_L12")
        s_T = sem("s_T")
        s_Th = sem("s_Th")
        s_Tl = sem("s_Tl")
        s_PV = sem("s_PV")
        s_Oh = sem("s_Oh")
        s_Ol = sem("s_Ol")
        s_y = sem("s_y")
        s_res = sem("s_res")
        s_w2 = sem("s_w2")
        s_w2T = sem("s_w2T")
        s_w2Tc = sem("s_w2Tc")
        s_tab = sem("s_tab")
        s_texp = sem("s_texp")
        s_tdve = sem("s_tdve")
        s_ln2 = sem("s_ln2")
        s_m = {n: sem("m_" + n) for n in ("xn", "xT", "xc", "tmp", "mix", "kvr", "ek", "er", "er1", "sum",
                                          "cs", "st", "o", "y", "res", "ch")}
        s_w3 = sem("s_w3")
        s_w3e = [sem(f"s_w3e{i}") for i in range(2)]
        s_w3T = sem("s_w3T")
        s_w3Tc = sem("s_w3Tc")
        s_f = {n: sem("f_" + n) for n in ("xn", "xT", "xc", "lg", "h", "hr", "y", "acc", "ch", "eq")}

        block = top.enter_context(nc.Block())

        arena = ExitStack()

        def asb(name, shape, dt=F32):
            return arena.enter_context(nc.sbuf_tensor(name, shape, dt))

        x1h = asb("x1h", [P, TOK], F16)
        x1l = asb("x1l", [P, TOK], F16)
        bob = asb("bob", [P, C])
        Ahi = asb("Ahi", [P, H, CC], F16)
        Alo = asb("Alo", [P, H, CC], F16)
        Bhi = asb("Bhi", [CC, H, C], F16)
        Blo = asb("Blo", [CC, H, C], F16)
        raw = asb("raw", [P, NP2, GB, MC + 1, CC])
        raw12 = asb("raw12", [LR, NP2, GB, CC])
        NC8 = NP2 * GB
        chi = asb("chi", [P, NC8, MC + 1, CC], F16)
        clo = asb("clo", [P, NC8, MC + 1, CC], F16)
        h12 = asb("h12", [LR, GB, CC], F16)
        g12 = asb("g12", [LR, GB, CC], F16)
        c3 = asb("c3", [LR, GB, CC], F16)
        Z = asb("Z", [LR, NP2, GB, QT, CC], F16)
        zmask = asb("zmask", [LR, QT])
        nlo = asb("nlo", [LR, 1])
        MP = M + 1
        cT = asb("cT", [CC, 4, 2, MP], F16)
        qh = asb("qh", [CC, NP2, GB, Q], F16)
        ql = asb("ql", [CC, NP2, GB, Q], F16)
        nmax = asb("nmax", [P, NP2, QT])
        sums = asb("sums", [P, NP2, QT])
        rsum = asb("rsum", [P, NP2, QT])
        Pe = asb("Pe", [P, NP2, QT, M])
        Pn = asb("Pn", [P, NP2, QT, M])
        e12 = asb("e12", [P, NP2, R3, QT], F16)
        Th = asb("Th", [P, NP2, MC, Q], F16)
        Tl = asb("Tl", [P, NP2, MC, Q], F16)
        L12 = asb("L12", [LR, NP2, P], F16)
        Oh = asb("Oh", [CC, NP2, H, P], F16)
        Ol = asb("Ol", [CC, NP2, H, P], F16)
        warena = ExitStack()
        wq_r = warena.enter_context(nc.sbuf_tensor("wq_r", [P, HD], F32))
        wk_r = warena.enter_context(nc.sbuf_tensor("wk_r", [CC, HD], F32))
        wv_r = warena.enter_context(nc.sbuf_tensor("wv_r", [CC, HD], F32))
        wo_r = warena.enter_context(nc.sbuf_tensor("wo_r", [P, H // 2, C], F32))
        wqT = warena.enter_context(nc.sbuf_tensor("wqT", [P, H // 2, P], F32))
        wkT = warena.enter_context(nc.sbuf_tensor("wkT", [P, H // 2, CC], F32))
        wvT = warena.enter_context(nc.sbuf_tensor("wvT", [P, H // 2, CC], F32))
        warena.close()
        arena.close()

        late = ExitStack()

        def lsb(name, shape, dt=F32):
            return late.enter_context(nc.sbuf_tensor(name, shape, dt))

        w2r = lsb("w2r", [P, 4, C])
        w2T = lsb("w2T", [P, 4, C])
        mix = lsb("mix", [P, 3])
        omm = lsb("omm", [P, 3])
        dcy = lsb("dcy", [P, 2])
        nlw = lsb("nlw", [P, 2])
        nlw2 = lsb("nlw2", [P, 2])
        tt = lsb("tt", [P, N + 1])
        apw = lsb("apw", [P, N + 1])
        iap = lsb("iap", [P, N + 1])
        blk = lsb("blk", [P, P])
        onesn = lsb("onesn", [P, N])
        xT33 = lsb("xT33", [P, SEQ, N + 1])
        tmp3 = lsb("tmp3", [P, 3, T])
        xm3 = lsb("xm3", [P, 3, T])
        ek = lsb("ek", [P, T])
        er = lsb("er", [P, T])
        dmx = lsb("dmx", [P, T])
        ekv = lsb("ekv", [P, T])
        fab = lsb("fab", [P, 2, T])
        cs = lsb("cs", [P, 2, SEQ, N + 1])
        sraw = lsb("sraw", [P, 2, T])
        scl = lsb("scl", [P, 2, T])
        sst = lsb("sst", [P, 2, T])
        num = lsb("num", [P, T])
        den = lsb("den", [P, T])
        rec = lsb("rec", [P, T])
        oT = lsb("oT", [P, T])
        w1r = lsb("w1r", [P, 2, FC, C])
        w2fr = lsb("w2fr", [P, 2, FF])
        W1T = lsb("W1T", [P, E, FF])
        W2T = lsb("W2T", [P, E, FC, C])
        wrr = lsb("wrr", [E, C])
        wrT = lsb("wrT", [P, E])
        brb = lsb("brb", [P, E])
        b1r = lsb("b1r", [E * FC, P])
        b1T = lsb("b1T", [P, E * FC])
        b2r = lsb("b2r", [1, E * C])
        ones1 = lsb("ones1", [1, P])
        desc = lsb("desc", [P, E])
        x3T = lsb("x3T", [P, T])
        lg = lsb("lg", [P, CT, E])
        eq = lsb("eq", [P, CT, E])
        wt = lsb("wt", [P, CT, E])
        mx = lsb("mx", [P, CT])
        hb = lsb("hb", [P, 2, FC, T])
        late.close()

        bankh = [b[:, :].bitcast(F16) for b in bank]

        xt_dram = x.rearrange("(g b) n c -> (b n) g c", b=GB)
        out_dram = out.rearrange("(g b) n c -> (b n) g c", b=GB)
        ctx_main = ctx[:, 0:MC * P, :].rearrange("b (p s) c -> p b s c", s=MC)
        col = lambda a: a.rearrange("a b c -> c (a b)")

        def heads(buf, k):
            return buf[:, :, :].rearrange("p (q two) c -> p two q c", two=2)[:, k % 2, 4 * (k // 2):4 * (k // 2) + 4, :]


        def where(it, j):
            return 8 * it + j, 2 * it + j // GB, j % GB, (j // GB) % NP2

        def pe_ctxT(n, s8, s4):
            wait(nc.tensor, s_clo, n + 1)
            wait(nc.tensor, s_cT, n)
            wait(nc.tensor, s_L12, n - 2)
            for half, src in enumerate((chi, clo)):
                for c in range(MC):
                    nc.tensor.transpose(bankh[7][0:CC, half * MP + c * P:half * MP + (c + 1) * P],
                                        src[:, s8, c, :], ident[:, :])
                last = nc.tensor.transpose(bankh[7][0:CC, half * MP + MC * P:half * MP + MC * P + 2],
                                           src[0:2, s8, MC, :], ident[0:2, 0:2])
            last.then_inc(s_ctxT, 1)

        def pe_scores(n, par, b, s4):
            g = n // GB if isinstance(n, int) else None
            wait(nc.tensor, s_cT, n + 1)
            for t in range(QT):
                wait(nc.tensor, s_exp, QT * (n - 1) + t + 1)
                for k, (w, c) in enumerate(((qh, 0), (qh, 1), (ql, 0))):
                    last = nc.tensor.matmul(bank[t][:, 0:M], w[:, par, b, t * P:(t + 1) * P],
                                            cT[:, s4, c, 0:M], start=(k == 0), stop=(k == 2))
                last.then_inc(s_S, 1)

        def pe_q(g, c, tok):
            for hh in range(QT):
                h = QT * c + hh
                for k, (w, a) in enumerate(((Ahi, x1h), (Ahi, x1l), (Alo, x1h))):
                    last = nc.tensor.matmul(bank[7][0:CC, hh * P:(hh + 1) * P], w[:, h, :], a[:, tok],
                                            start=(k == 0), stop=(k == 2))
            last.then_inc(s_q, 1)

        def pe_pv(n, par, s8, gp, b):
            wait(nc.tensor, s_Ol, n)
            k = 0
            for w, p, s in ((chi, Th, s_Th), (clo, Th, None), (chi, Tl, s_Tl)):
                for c in range(MC):
                    if s is not None:
                        wait(nc.tensor, s, MC * n + c + 1)
                    nc.tensor.matmul(bank[6][0:CC, :], w[:, s8, c, :], p[:, par, c, :], start=(k == 0), stop=False)
                    k += 1
            wait(nc.tensor, s_L12, n + 1)
            for t in range(QT):
                last = nc.tensor.matmul(bank[6][0:CC, t * P:(t + 1) * P], Z[:, gp, b, t, :], L12[:, par, :],
                                        start=False, stop=(t == QT - 1))
            last.then_inc(s_PV, 1)

        def pe_y(g, gp):
            wait(nc.tensor, s_Ol, GB * (g + 1))
            for h in range(H):
                for k, (o, w) in enumerate(((Oh, Bhi), (Oh, Blo), (Ol, Bhi))):
                    last = nc.tensor.matmul(bank[7][:, 0:C], o[:, gp, h, :], w[:, h, :],
                                            start=(h == 0 and k == 0), stop=(h == H - 1 and k == 2))
            last.then_inc(s_y, 1)

        def pe_probsT(n, par):
            for c in range(MC):
                wait(nc.tensor, s_Tl, MC * (n - 1) + c + 1)
                for t in range(QT):
                    last = nc.tensor.transpose(bank[4 + c][:, t * P:(t + 1) * P], Pn[:, par, t, c * P:(c + 1) * P],
                                               identf[:, :])
                last.then_inc(s_T, 1)

        def exists(n, last=B):
            return not isinstance(n, int) or 0 <= n < last

        def pe_step(it, j):
            n, g, jj, gp = where(it, j)
            if exists(n + 2):
                pe_ctxT(n + 2, (j + 2) % NC8, (j + 2) % 4)
            if exists(n + 1):
                if (j + 1) % GB == 0:
                    wait(nc.tensor, s_ql, QT * ((n + 1) // GB + 1) if isinstance(n, int) else QT * (2 * it + (j + 1) // GB + 1))
                pe_scores(n + 1, ((j + 1) // GB) % NP2, (j + 1) % GB, (j + 1) % 4)
            queries = exists(n) and jj in (0, 1) and exists(g + 1, G)
            if queries:
                wait(nc.tensor, s_cT, n + 3)
                pe_q(g + 1, 2 * jj, bass.ds(P * (g + 1), P))
            if jj == 2 and exists(g - 1, G):
                if exists(n + 2):
                    wait(nc.tensor, s_cT, n + 3)
                else:
                    wait(nc.tensor, s_L12, min(n, B))
                pe_y(g - 1, 1 - gp)
            if exists(n - 1):
                pe_pv(n - 1, (j - 1) % NP2, (j - 1) % NC8, ((j - 1) // GB) % NP2, (j - 1) % GB)
            if queries:
                wait(nc.tensor, s_ql, QT * (g + 1) + 2 * jj + 1)
                pe_q(g + 1, 2 * jj + 1, bass.ds(P * (g + 1), P))
            if exists(n):
                if queries:
                    wait(nc.tensor, s_ql, QT * (g + 1) + 2 * jj + 2)
                elif jj == 2 and exists(g - 1, G):
                    wait(nc.tensor, s_res, g)
                else:
                    wait(nc.tensor, s_cT, min(n + 3, B) if isinstance(n, int) else n + 3)
                wait(nc.tensor, s_elo, n + 1)
                nc.tensor.transpose(bankh[7][0:LR, 0:P], e12[:, n_par(j), :, :].rearrange("p r t -> p (r t)"),
                                    ident[:, :]).then_inc(s_left, 1)
                wait(nc.tensor, s_pn, n + 1)
                pe_probsT(n, n_par(j))

        def n_par(j):
            return j % NP2

        def act_step(it, j):
            n, g, jj, gp = where(it, j)
            if exists(n - 1):
                wait(nc.scalar, s_PV, n - 2)
                for c in range(MC):
                    wait(nc.scalar, s_T, MC * (n - 1) + c + 1)
                    nc.scalar.activation(Th[:, n_par(j - 1), c, :], bank[4 + c][:, :], ACT.Copy).then_inc(s_Th, 1)
            if exists(n + 1):
                wait(nc.scalar, s_elo, n)
                for t in range(QT):
                    wait(nc.scalar, s_nmax, 2 * (n + 1) + t // 2 + 1)
                    nc.scalar.activation(Pe[:, n_par(j + 1), t, :], bank[t][:, 0:M], ACT.Exp,
                                         bias=nmax[:, n_par(j + 1), t:t + 1],
                                         accum_out=sums[:, n_par(j + 1), t:t + 1]).then_inc(s_exp, 1)
            queries = exists(n) and jj in (0, 1) and exists(g + 1, G)
            if queries:
                act_q(QT * (g + 1) + 2 * jj, 1 - gp, 2 * jj)
            if exists(n - 1):
                if (j - 1) % GB == 0:
                    wait(nc.scalar, s_y, g - 1)
                wait(nc.scalar, s_PV, n)
                nc.scalar.activation(Oh[:, ((j - 1) // GB) % NP2, :, ((j - 1) % GB) * N:((j - 1) % GB + 1) * N],
                                     bank[6][0:CC, :].rearrange("p (h t) -> p h t", h=H), ACT.Copy).then_inc(s_Oh, 1)
            if queries:
                act_q(QT * (g + 1) + 2 * jj + 1, 1 - gp, 2 * jj + 1)

        def q_view(buf, par, c):
            return buf[:, par, :, c * P:(c + 1) * P].rearrange("p b (h t) -> p h b t", h=QT)

        def act_q(k, par, c):
            wait(nc.scalar, s_q, k + 1)
            wait(nc.scalar, s_S, QT * (k - c) - QT * GB)
            nc.scalar.activation(q_view(qh, par, c), bank[7][0:CC, :].rearrange("p (h b t) -> p h b t", h=QT, b=GB),
                                 ACT.Copy).then_inc(s_qh, 1)

        def dve_q(k, par, c):
            wait(nc.vector, s_qh, k + 1)
            nc.vector.tensor_tensor(q_view(ql, par, c), bank[7][0:CC, :].rearrange("p (h b t) -> p h b t", h=QT, b=GB),
                                    q_view(qh, par, c), ALU.subtract).then_inc(s_ql, 1)

        def dve_step(it, j):
            n, g, jj, gp = where(it, j)
            if exists(n + 2):
                dve_cT(n + 2, (j + 2) % 4)
            if exists(n - 1):
                for c in range(MC):
                    wait(nc.vector, s_Th, MC * (n - 1) + c + 1)
                    nc.vector.tensor_tensor(Tl[:, n_par(j - 1), c, :], bank[4 + c][:, :], Th[:, n_par(j - 1), c, :],
                                            ALU.subtract).then_inc(s_Tl, 1)
            if exists(n + 1):
                for u in range(2):
                    wait(nc.vector, s_S, QT * (n + 1) + 2 * u + 2)
                    for t in (2 * u, 2 * u + 1):
                        last = nc.vector.tensor_reduce(nmax[:, n_par(j + 1), t:t + 1], bank[t][:, 0:M], AX.X, ALU.max,
                                                       negate=True)
                    last.then_inc(s_nmax, 1)
            queries = exists(n) and jj in (0, 1) and exists(g + 1, G)
            if queries:
                dve_q(QT * (g + 1) + 2 * jj, 1 - gp, 2 * jj)
            if jj == 2 and exists(g - 1, G):
                wait(nc.vector, s_y, g)
                tile = X[:, bass.ds(g - 1, 1), :].rearrange("p o c -> p (o c)")
                nc.vector.tensor_tensor(tile, tile, bank[7][:, 0:C], ALU.add).then_inc(s_res, 1)
            if exists(n - 1):
                wait(nc.vector, s_Oh, n)
                sl = (slice(None), ((j - 1) // GB) % NP2, slice(None), slice(((j - 1) % GB) * N, ((j - 1) % GB + 1) * N))
                nc.vector.tensor_tensor(Ol[sl], bank[6][0:CC, :].rearrange("p (h t) -> p h t", h=H), Oh[sl],
                                        ALU.subtract).then_inc(s_Ol, 1)
            if exists(n + 1):
                wait(nc.vector, s_exp, QT * (n + 2))
                wait(nc.vector, s_pn, n)
                nc.vector.reciprocal(rsum[:, n_par(j + 1), :], sums[:, n_par(j + 1), :]).then_inc(s_rs, 1)
            if queries:
                dve_q(QT * (g + 1) + 2 * jj + 1, 1 - gp, 2 * jj + 1)
            if exists(n):
                wait(nc.vector, s_left, n + 1)
                wait(nc.vector, s_PV, n - 1)
                nc.vector.tensor_copy(L12[:, n_par(j), :], bankh[7][0:LR, 0:P]).then_inc(s_L12, 1)

        def dve_cT(n, s4):
            wait(nc.vector, s_ctxT, n + 1)
            nc.vector.tensor_copy(cT[:, s4, :, :].rearrange("p s m -> p (s m)"), bankh[7][0:CC, 0:2 * MP])\
                .then_inc(s_cT, 1)

        def pool_prep(n, s8, par, b):
            wait(nc.gpsimd, s_PV, n - 7)
            nc.gpsimd.tensor_tensor(chi[:, s8, :, :], raw[:, par, b, :, :],
                                    one[:, 0:1].unsqueeze(2).broadcast_to([P, MC + 1, CC]), ALU.mult)\
                .then_inc(s_chi, 1)
            wait(nc.gpsimd, s_chi, n + 1)
            nc.gpsimd.tensor_tensor(clo[:, s8, :, :], raw[:, par, b, :, :], chi[:, s8, :, :], ALU.subtract)\
                .then_inc(s_clo, 1)

        def pool_z(g, par):
            nc.gpsimd.tensor_tensor(h12[:, :, :], raw12[:, par, :, :],
                                    one[0:LR, 0:1].unsqueeze(2).broadcast_to([LR, GB, CC]), ALU.mult).then_inc(s_h12, 1)
            wait(nc.gpsimd, s_h12, g + 1)
            nc.gpsimd.tensor_tensor(g12[:, :, :], h12[:, :, :], nlo[:, 0:1].unsqueeze(2).broadcast_to([LR, GB, CC]),
                                    ALU.mult).then_inc(s_g12, 1)
            wait(nc.gpsimd, s_g12, g + 1)
            nc.gpsimd.tensor_tensor(c3[:, :, :], g12[:, :, :], raw12[:, par, :, :], ALU.add).then_inc(s_c3, 1)
            wait(nc.gpsimd, s_c3, g + 1)
            wait(nc.gpsimd, s_PV, GB * (g - 1))
            for b in range(GB):
                last = nc.gpsimd.tensor_tensor(Z[:, par, b, :, :], c3[:, b:b + 1, :].broadcast_to([LR, QT, CC]),
                                               zmask[:, :].unsqueeze(2).broadcast_to([LR, QT, CC]), ALU.mult)
            last.then_inc(s_z, 1)

        def pool_step(it, j):
            n, g, jj, gp = where(it, j)
            if exists(n + 4):
                if (j + 4) % GB == 0:
                    gn = g + 1 if j >= 0 else 0
                    wait(nc.gpsimd, s_ctx[((j + 4) // GB) % NP2], 48 * (it + 1 + ((j + 4) // GB - ((j + 4) // GB) % NP2) // NP2))
                pool_prep(n + 4, (j + 4) % NC8, ((j + 4) // GB) % NP2, (j + 4) % GB)
            if exists(n + 1):
                wait(nc.gpsimd, s_rs, n + 2)
                wait(nc.gpsimd, s_T, MC * n)
                par = n_par(j + 1)
                nc.gpsimd.tensor_tensor(Pn[:, par, :, :], Pe[:, par, :, :],
                                        rsum[:, par, :].unsqueeze(2).broadcast_to([P, QT, M]), ALU.mult)\
                    .then_inc(s_pn, 1)
                wait(nc.gpsimd, s_pn, n + 2)
                wait(nc.gpsimd, s_left, n)
                lastcol = Pn[:, par, :, LAST:M].rearrange("p t o -> p (t o)")
                for r in (0, 2):
                    last = nc.gpsimd.tensor_tensor(e12[:, par, r, :], lastcol,
                                                   one[:, 0:1].broadcast_to([P, QT]), ALU.mult)
                last.then_inc(s_ehi, 1)
                wait(nc.gpsimd, s_ehi, n + 2)
                nc.gpsimd.tensor_tensor(e12[:, par, 1, :], lastcol, e12[:, par, 0, :], ALU.subtract).then_inc(s_elo, 1)
            if jj == 2 and exists(g + 1, G):
                pool_z(g + 1, 1 - gp)

        def pipeline(eng, step):
            for j in range(-1, 7):
                step(0, j)
            with eng.Fori(1, B // 8 - 1) as it:
                for j in range(-1, 7):
                    step(it, j)
            for j in range(-1, 11):
                step(B // 8 - 1, j)

        def over_chunks(eng):
            def run(body):
                body(0)
                with eng.Fori(1, CH) as i:
                    body(i)
            return run

        LS = G + 6 + 5

        def dve_stats(chain, base):
            @over_chunks(nc.vector)
            def _(i):
                for t in range(CT):
                    nc.vector.bn_stats(stats[:, bass.ds(CT * i + t, 1), :].rearrange("p o s -> p (o s)"),
                                       X[:, bass.ds(CT * i + t, 1), :].rearrange("p o c -> p (o c)"))\
                        .then_inc(chain.sem, 1)
            chain.at(base + G)
            nc.vector.wait_ge(chain.sem, base + G)
            chain.mark(nc.vector.tensor_tensor(tmpv[:, :], stats[:, :, 1], stats[:, :, 4], ALU.add))
            chain.mark(nc.vector.tensor_tensor(std[:, :], stats[:, :, 1], stats[:, :, 4], ALU.subtract))
            chain.link(nc.vector.tensor_tensor(rst[:, :], stats[:, :, 2], stats[:, :, 5], ALU.add))
            chain.mark(nc.vector.tensor_scalar(mean[:, :], tmpv[:, :], 0.5, None, ALU.mult))
            chain.link(nc.vector.scalar_tensor_tensor(varp[:, :], std[:, :], 0.25, std[:, :], ALU.mult, ALU.mult))
            chain.link(nc.vector.tensor_scalar(tmpv[:, :], rst[:, :], 1.0 / C, EPS, ALU.mult, ALU.add))

        def dve_rstd(chain, phase):
            nc.vector.tensor_tensor(varp[:, :], varp[:, :], tmpv[:, :], ALU.add).then_inc(s_var, 1)
            nc.vector.wait_ge(s_var, phase)
            nc.vector.wait_ge(s_std, phase)
            chain.link(nc.vector.reciprocal(rst[:, :], std[:, :]))
            chain.link(nc.vector.tensor_tensor(tmpv[:, :], rst[:, :], rst[:, :], ALU.mult))
            chain.link(nc.vector.tensor_tensor(tmpv[:, :], tmpv[:, :], varp[:, :], ALU.mult))
            chain.link(nc.vector.tensor_scalar(tmpv[:, :], tmpv[:, :], -0.5, 1.5, ALU.mult, ALU.add))
            chain.link(nc.vector.tensor_tensor(rst[:, :], rst[:, :], tmpv[:, :], ALU.mult))

        def act_std(phase):
            nc.scalar.wait_ge(s_var, phase)
            nc.scalar.activation(std[:, :], varp[:, :], ACT.Sqrt).then_inc(s_std, 1)

        def dve_norm(i, par, s):
            for t in range(CT):
                k = CT * i + t
                last = nc.vector.tensor_scalar(xn[:, par, t, :], X[:, bass.ds(k, 1), :].rearrange("p o c -> p (o c)"),
                                               mean[:, bass.ds(k, 1)],
                                               rst[:, bass.ds(k, 1)], ALU.subtract, ALU.mult)
            last.then_inc(s, 1)

        def pe_norm_T(par, b, s):
            for t in range(CT):
                last = nc.tensor.transpose(bank[b][:, t * P:(t + 1) * P], xn[:, par, t, :], identf[:, :])
            last.then_inc(s, 1)

        @block.sync
        def _(sp):
            sp.dma_start(X[:, :, :], xt_dram).then_inc(s_x, 16)
            sp.dma_start(wq_r[:, :], Wq).then_inc(s_w, 16)
            sp.dma_start(wk_r[:, :], Wk).then_inc(s_w, 16)
            sp.dma_start(wv_r[:, :], Wv).then_inc(s_w, 16)
            sp.dma_start(wo_r[:, :, :], Wo.rearrange("(a p) c -> p a c", p=P)).then_inc(s_w, 16)
            sp.dma_start(bob[:, :], bo.rearrange("(o c) -> o c", o=1).broadcast_to([P, C])).then_inc(s_bo, 16)
            sp.wait_ge(s_raw0, 1)

            def load_ctx(g, par):
                b0 = GB * g
                wait(sp, s_clo, GB * (g - 1))
                wait(sp, s_c3, g - 1)
                sp.dma_start(raw[:, par, :, 0:MC, :], ctx_main[:, bass.ds(b0, GB), :, :]).then_inc(s_ctx[par], 16)
                lastrow = ctx[bass.ds(b0, GB), LAST:M, :].rearrange("b o c -> o b c")
                sp.dma_start(raw[0:1, par, :, MC, :], lastrow).then_inc(s_ctx[par], 16)
                sp.dma_start(raw12[:, par, :, :], lastrow.broadcast_to([LR, GB, CC])).then_inc(s_ctx[par], 16)

            load_ctx(0, 0)
            load_ctx(1, 1)
            with sp.Fori(1, G // 2) as i:
                load_ctx(2 * i, 0)
                load_ctx(2 * i + 1, 1)

            sp.wait_ge(s_res, G)
            for i, w in enumerate((W_key, W_value, W_rec, W_out)):
                sp.dma_start(w2r[:, i, :], w).then_inc(s_w2, 16)
            for i, m in enumerate((mix_k, mix_v, mix_r)):
                sp.dma_start(mix[:, i:i + 1], col(m)).then_inc(s_w2, 16)
            for i, v in enumerate((decay, first)):
                for a in range(HS):
                    sp.dma_start(dcy[a:P:HS, i:i + 1], v.rearrange("(h o) -> h o", o=1)).then_inc(s_w2, 16)
            sp.dma_start(wrr[:, :], Wr).then_inc(s_w3, 16)
            sp.dma_start(brb[:, :], br.rearrange("(o e) -> o e", o=1).broadcast_to([P, E])).then_inc(s_w3, 16)
            sp.dma_start(b1r[:, :], b1.rearrange("e (f p) -> (e f) p", p=P)).then_inc(s_w3, 16)
            sp.dma_start(b2r[:, :], b2.rearrange("(o e) d -> o (e d)", o=1)).then_inc(s_w3, 16)
            for e in range(E):
                if e >= 2:
                    sp.wait_ge(s_w3T, 1 + 2 * (e - 1))
                sp.dma_start(w1r[:, e % 2, :, :], W1[e].rearrange("(f p) d -> p f d", p=P)).then_inc(s_w3e[e % 2], 16)
                sp.dma_start(w2fr[:, e % 2, :], W2[e]).then_inc(s_w3e[e % 2], 16)
            @over_chunks(sp)
            def _(i):
                sp.wait_ge(s_f["acc"], E * (i + 1))
                sp.dma_start(out_dram[:, bass.ds(CT * i, CT), :], X[:, bass.ds(CT * i, CT), :]).then_inc(s_out, 16)
            sp.wait_ge(s_out, 16 * CH)

        @block.gpsimd
        def _(pool):
            nc.gpsimd.memset(identf[:, :], 0.0).then_inc(s_id, 1)
            nc.gpsimd.memset(zmask[:, :], 0.0).then_inc(s_id, 1)
            nc.gpsimd.memset(nlo[:, :], -1.0).then_inc(s_id, 1)
            nc.gpsimd.memset(one[:, :], 1.0).then_inc(s_id, 1)
            nc.gpsimd.memset(raw[:, :, :, MC, :], 0.0).then_inc(s_raw0, 1)
            pool.wait_ge(s_id, 4)
            nc.gpsimd.affine_select(out=identf[:, :], in_=identf[:, :], compare_op=ALU.not_equal, fill=1.0,
                                    base=0, pattern=[[-1, P]], channel_multiplier=1).then_inc(s_const, 1)
            nc.gpsimd.affine_select(out=nlo[:, :], in_=nlo[:, :], compare_op=ALU.is_ge, fill=0.0,
                                    base=-2 * QT, pattern=[[0, 1]], channel_multiplier=1).then_inc(s_const, 1)
            for r in range(R3):
                nc.gpsimd.affine_select(out=zmask[:, :], in_=zmask[:, :], compare_op=ALU.not_equal, fill=1.0,
                                        base=-QT * r, pattern=[[-1, QT]], channel_multiplier=1).then_inc(s_const, 1)
                pool.wait_ge(s_const, 3 + r)
            nc.gpsimd.tensor_copy(ident[:, :], identf[:, :]).then_inc(s_const, 1)
            pool.wait_ge(s_const, 3 + R3)
            pool.wait_ge(s_ctx[0], 48)
            pool_z(0, 0)
            for b in range(GB - 1):
                pool_prep(b, b, 0, b)
            pool.wait_ge(s_bo, 16)
            pool.wait_ge(s_xn1, CH)
            nc.gpsimd.tensor_tensor(X[:, :, :], X[:, :, :], bob[:, :].unsqueeze(1).broadcast_to([P, G, C]), ALU.add)\
                .then_inc(s_bo, 1)
            pipeline(nc.gpsimd, pool_step)

            pool.wait_ge(s_res, G)
            nc.gpsimd.iota(tt[:, :], pattern=[[1, N + 1]], base=0, channel_multiplier=0,
                           allow_small_or_imprecise_dtypes=True).then_inc(s_tab, 1)
            nc.gpsimd.iota(desc[:, :], pattern=[[-1, E]], base=E, channel_multiplier=0,
                           allow_small_or_imprecise_dtypes=True).then_inc(s_tab, 1)
            nc.gpsimd.memset(xT33[:, :, :], 0.0).then_inc(s_tab, 1)
            nc.gpsimd.memset(cs[:, :, :, :], 0.0).then_inc(s_tab, 1)
            nc.gpsimd.memset(ones1[:, :], 1.0).then_inc(s_tab, 1)
            nc.gpsimd.memset(onesn[:, :], 1.0).then_inc(s_tab, 1)
            nc.gpsimd.memset(blk[:, :], 1.0).then_inc(s_tab, 1)
            pool.wait_ge(s_tab, 7)
            bv = blk[:, :].rearrange("p (h a) -> p h a", a=HS)
            nc.gpsimd.affine_select(out=bv, in_=bv, compare_op=ALU.is_ge, fill=0.0, base=0,
                                    pattern=[[-HS, H], [0, HS]], channel_multiplier=1).then_inc(s_tab, 1)
            pool.wait_ge(s_tab, 8)
            nc.gpsimd.affine_select(out=bv, in_=bv, compare_op=ALU.is_ge, fill=0.0, base=HS - 1,
                                    pattern=[[HS, H], [0, HS]], channel_multiplier=-1).then_inc(s_tab, 1)
            @over_chunks(nc.gpsimd)
            def _(i):
                pool.wait_ge(s_tdve, 1)
                pool.wait_ge(s_m["xc"], i + 1)
                for k in range(3):
                    last = nc.gpsimd.tensor_tensor(tmp3[:, k, :].rearrange("p (s n) -> p s n", n=N), xT33[:, :, 0:N],
                                                   omm[:, k:k + 1].unsqueeze(2).broadcast_to([P, SEQ, N]), ALU.mult)
                last.then_inc(s_m["tmp"], 1)
                for k in range(2):
                    pool.wait_ge(s_m["cs"], 2 * i + k + 1)
                    nc.gpsimd.tensor_tensor(sraw[:, k, :].rearrange("p (s n) -> p s n", n=N), cs[:, k, :, 0:N],
                                            apw[:, 0:N].unsqueeze(1).broadcast_to([P, SEQ, N]), ALU.mult)\
                        .then_inc(s_m["st"], 1)

        @block.scalar
        def _(act):
            act_std(1)
            for k in range(6):
                act.wait_ge(s_wT, k + 1)
                dst, w = ((wqT, P), (wkT, CC), (wvT, CC))[k // 2]
                nc.scalar.activation(dst[:, 4 * (k % 2):4 * (k % 2) + 4, :],
                                     bank[k % 2][:, 0:4 * w].rearrange("p (a c) -> p a c", a=4), ACT.Copy)\
                    .then_inc(s_wTc, 1)
            for k in range(8):
                act.wait_ge(s_ab, k + 1)
                if k < 4:
                    nc.scalar.activation(heads(Ahi, k),
                                         bank[2 + k % 2][:, 0:4 * CC].rearrange("p (a c) -> p a c", a=4), ACT.Copy,
                                         scale=SCALE).then_inc(s_abh, 1)
                else:
                    nc.scalar.activation(heads(Bhi, k - 4),
                                         bank[2 + k % 2][0:CC, :].rearrange("p (a c) -> p a c", a=4), ACT.Copy)\
                        .then_inc(s_abh, 1)
            @over_chunks(act)
            def _(i):
                act.wait_ge(s_x1T, i + 1)
                nc.scalar.activation(x1h[:, bass.ds(T * i, T)], bank[4][:, :], ACT.Copy).then_inc(s_x1h, 1)
            for c in range(QT):
                act_q(c, 0, c)
            pipeline(nc.scalar, act_step)

            act_std(2)
            act.wait_ge(s_w2T, 1)
            nc.scalar.activation(w2T[:, :, :].rearrange("p a c -> p (a c)"), bank[1][:, :], ACT.Copy).then_inc(s_w2Tc, 1)
            act.wait_ge(s_w2, 16 * (7 + 2 * HS))
            nc.scalar.activation(nlw[:, :], dcy[:, :], ACT.Exp).then_inc(s_texp, 1)
            act.wait_ge(s_tdve, 1)
            act.wait_ge(s_tab, 1)
            nc.scalar.activation(apw[:, :], tt[:, :], ACT.Exp, scale=nlw2[:, 0:1])\
                .then_inc(s_texp, 1)
            @over_chunks(act)
            def _(i):
                act.wait_ge(s_m["xT"], i + 1)
                wait(act, s_m["mix"], i)
                nc.scalar.activation(xT33[:, :, 1:N + 1], bank[0][:, :].rearrange("p (s n) -> p s n", n=N), ACT.Copy)\
                    .then_inc(s_m["xc"], 1)
                act.wait_ge(s_m["kvr"], 3 * i + 1)
                wait(act, s_m["res"], i)
                nc.scalar.activation(ek[:, :], bank[1][:, :], ACT.Exp).then_inc(s_m["ek"], 1)
                act.wait_ge(s_m["kvr"], 3 * i + 3)
                nc.scalar.activation(er[:, :], bank[3][:, :], ACT.Exp, scale=-1.0).then_inc(s_m["er"], 1)

            act_std(3)
            act.wait_ge(s_w3T, 1)
            nc.scalar.activation(wrT[:, :], bank[0][:, 0:E], ACT.Copy).then_inc(s_w3Tc, 1)
            nc.scalar.activation(b1T[:, :], bank[0][:, E:E + E * FC], ACT.Copy).then_inc(s_w3Tc, 1)
            for e in range(E):
                act.wait_ge(s_w3T, 2 + 2 * e)
                nc.scalar.activation(W1T[:, e, :], bank[1][:, :], ACT.Copy).then_inc(s_w3Tc, 1)
                act.wait_ge(s_w3T, 3 + 2 * e)
                nc.scalar.activation(W2T[:, e, :, :].rearrange("p f c -> p (f c)"), bank[2][:, :], ACT.Copy)\
                    .then_inc(s_w3Tc, 1)
            act.wait_ge(s_w3Tc, 2 + 2 * E)
            @over_chunks(act)
            def _(i):
                act.wait_ge(s_f["xT"], i + 1)
                wait(act, s_f["y"], E * i)
                nc.scalar.activation(x3T[:, :], bank[0][:, :], ACT.Copy).then_inc(s_f["xc"], 1)
                for e in range(E):
                    if e >= 2:
                        act.wait_ge(s_f["y"], E * i + e - 1)
                    for f in range(FC):
                        act.wait_ge(s_f["h"], E * FC * i + FC * e + f + 1)
                        nc.scalar.activation(hb[:, e % 2, f, :], bank[2 + f][:, :], ACT.Relu,
                                             bias=b1T[:, FC * e + f:FC * e + f + 1]).then_inc(s_f["hr"], 1)

        @block.tensor
        def _(pe):
            pe.wait_ge(s_const, 3 + R3)
            pe.wait_ge(s_w, 16 * 4)
            for k in range(6):
                src, w = ((wq_r, P), (wk_r, CC), (wv_r, CC))[k // 2]
                wait(pe, s_wTc, k - 1)
                for a in range(4):
                    p = 4 * (k % 2) + a
                    last = nc.tensor.transpose(bank[k % 2][:, a * w:(a + 1) * w], src[:, p * P:(p + 1) * P],
                                               identf[0:w, 0:w])
                last.then_inc(s_wT, 1)
            pe.wait_ge(s_wTc, 6)
            for k in range(8):
                wait(pe, s_abl, k - 1)
                for a in range(4):
                    lo, pair = (k % 2) * D, (k % 4) // 2 * 4 + a
                    if k < 4:
                        last = nc.tensor.matmul(bank[2 + k % 2][:, a * CC:(a + 1) * CC], wqT[lo:lo + D, pair, :],
                                                wkT[lo:lo + D, pair, :], start=True, stop=True)
                    else:
                        last = nc.tensor.matmul(bank[2 + k % 2][0:CC, a * C:(a + 1) * C], wvT[lo:lo + D, pair, :],
                                                wo_r[lo:lo + D, pair, :], start=True, stop=True)
                last.then_inc(s_ab, 1)
            @over_chunks(pe)
            def _(i):
                pe.wait_ge(s_xn1, i + 1)
                wait(pe, s_x1l, i)
                pe_norm_T(0, 4, s_x1T)
            pe.wait_ge(s_x1l, CH)
            pe.wait_ge(s_abl, 8)
            pe_ctxT(0, 0, 0)
            pe.wait_ge(s_cT, 1)
            for c in range(QT):
                wait(pe, s_ql, c)
                pe_q(0, c, slice(0, P))
            pe.wait_ge(s_ql, QT)
            pipeline(nc.tensor, pe_step)

            pe.wait_ge(s_res, G)
            pe.wait_ge(s_w2, 16 * (7 + 2 * HS))
            for a in range(4):
                last = nc.tensor.transpose(bank[1][:, a * P:(a + 1) * P], w2r[:, a, :], identf[:, :])
            last.then_inc(s_w2T, 1)
            pe.wait_ge(s_w2Tc, 1)
            pe.wait_ge(s_tab, 9)
            @over_chunks(pe)
            def _(i):
                pe.wait_ge(s_m["xn"], i + 1)
                pe_norm_T(0, 0, s_m["xT"])
                for k in range(3):
                    pe.wait_ge(s_m["mix"], i + 1)
                    nc.tensor.matmul(bank[1 + k][:, :], w2T[:, k, :], xm3[:, k, :], start=True, stop=True)\
                        .then_inc(s_m["kvr"], 1)
                pe.wait_ge(s_m["ek"], i + 1)
                nc.tensor.matmul(bank[4][:, :], blk[:, :], ek[:, :], start=True, stop=True).then_inc(s_m["sum"], 1)
                pe.wait_ge(s_m["o"], i + 1)
                for t in range(CT):
                    last = nc.tensor.matmul(bank[5][:, t * P:(t + 1) * P], oT[:, t * P:(t + 1) * P], w2T[:, 3, :],
                                            start=True, stop=True)
                last.then_inc(s_m["y"], 1)

            pe.wait_ge(s_w3, 16 * 4)
            pe.wait_ge(s_m["res"], CH)
            nc.tensor.transpose(bank[0][:, 0:E], wrr[:, :], identf[0:E, 0:E])
            nc.tensor.transpose(bank[0][:, E:E + E * FC], b1r[:, :], identf[0:E * FC, 0:E * FC]).then_inc(s_w3T, 1)
            for e in range(E):
                pe.wait_ge(s_w3e[e % 2], 32 * (e // 2 + 1))
                wait(pe, s_w3Tc, 2 + 2 * e if e else 0)
                for f in range(FC):
                    last = nc.tensor.transpose(bank[1][:, f * P:(f + 1) * P], w1r[:, e % 2, f, :], identf[:, :])
                last.then_inc(s_w3T, 1)
                for f in range(FC):
                    last = nc.tensor.transpose(bank[2][:, f * P:(f + 1) * P], w2fr[:, e % 2, f * P:(f + 1) * P],
                                               identf[:, :])
                last.then_inc(s_w3T, 1)
            pe.wait_ge(s_w3Tc, 2 + 2 * E)
            @over_chunks(pe)
            def _(i):
                pe.wait_ge(s_f["xn"], i + 1)
                pe_norm_T(0, 0, s_f["xT"])
                pe.wait_ge(s_f["xc"], i + 1)
                for t in range(CT):
                    last = nc.tensor.matmul(bank[1][:, t * E:(t + 1) * E], x3T[:, t * P:(t + 1) * P], wrT[:, :],
                                            start=True, stop=True)
                last.then_inc(s_f["lg"], 1)
                for e in range(E + 1):
                    if e < E:
                        for f in range(FC):
                            if e:
                                pe.wait_ge(s_f["hr"], E * FC * i + FC * (e - 1) + f + 1)
                            nc.tensor.matmul(bank[2 + f][:, :], W1T[:, e, f * P:(f + 1) * P], x3T[:, :],
                                             start=True, stop=True).then_inc(s_f["h"], 1)
                    if e:
                        y = e - 1
                        pe.wait_ge(s_f["hr"], E * FC * i + FC * e)
                        if y >= 2:
                            pe.wait_ge(s_f["acc"], E * i + y - 1)
                        for t in range(CT):
                            o = bank[6 + y % 2][:, t * P:(t + 1) * P]
                            for f in range(FC):
                                nc.tensor.matmul(o, hb[:, y % 2, f, t * P:(t + 1) * P], W2T[:, y, f, :],
                                                 start=(f == 0), stop=False)
                            last = nc.tensor.matmul(o, ones1[:, :], b2r[:, y * C:(y + 1) * C], start=False, stop=True)
                        last.then_inc(s_f["y"], 1)

        @block.vector
        def _(dve):
            chain = Chain(dve, s_ln)
            dve.wait_ge(s_x, 16)
            dve_stats(chain, 0)
            dve_rstd(chain, 1)
            for k in range(8):
                dve.wait_ge(s_abh, k + 1)
                if k < 4:
                    nc.vector.scalar_tensor_tensor(heads(Alo, k), bank[2 + k % 2][:, 0:4 * CC].rearrange("p (a c) -> p a c", a=4),
                                                   SCALE, heads(Ahi, k), ALU.mult, ALU.subtract).then_inc(s_abl, 1)
                else:
                    nc.vector.tensor_tensor(heads(Blo, k - 4), bank[2 + k % 2][0:CC, :].rearrange("p (a c) -> p a c", a=4),
                                            heads(Bhi, k - 4), ALU.subtract).then_inc(s_abl, 1)
            @over_chunks(dve)
            def _(i):
                wait(dve, s_x1T, i)
                dve_norm(i, 0, s_xn1)
                dve.wait_ge(s_x1h, i + 1)
                nc.vector.tensor_tensor(x1l[:, bass.ds(T * i, T)], bank[4][:, :], x1h[:, bass.ds(T * i, T)],
                                        ALU.subtract).then_inc(s_x1l, 1)
            dve_cT(0, 0)
            for c in range(QT):
                dve_q(c, 0, c)
            dve.wait_ge(s_bo, 17)
            pipeline(nc.vector, dve_step)

            dve.wait_ge(s_res, G)
            base = LS
            dve_stats(chain, base)
            dve_rstd(chain, 2)
            dve.wait_ge(s_w2, 16 * (7 + 2 * HS))
            chain.link(nc.vector.tensor_scalar(omm[:, :], mix[:, :], -1.0, 1.0, ALU.mult, ALU.add))
            dve.wait_ge(s_texp, 1)
            nc.vector.tensor_scalar(nlw2[:, :], nlw[:, :], -1.0, None, ALU.mult).then_inc(s_tdve, 1)
            dve.wait_ge(s_texp, 2)
            chain.link(nc.vector.reciprocal(iap[:, :], apw[:, :]))
            dve.wait_ge(s_tab, 9)
            m = Chain(dve, s_m["ch"])
            per = 12
            @over_chunks(dve)
            def _(i):
                m.at(per * i)
                dve_norm(i, 0, s_m["xn"])
                dve.wait_ge(s_m["tmp"], i + 1)
                for k in range(3):
                    last = nc.vector.scalar_tensor_tensor(xm3[:, k, :].rearrange("p (s n) -> p s n", n=N),
                                                          xT33[:, :, 1:N + 1], mix[:, k:k + 1],
                                                          tmp3[:, k, :].rearrange("p (s n) -> p s n", n=N),
                                                          ALU.mult, ALU.add)
                last.then_inc(s_m["mix"], 1)
                v3 = lambda a: a.rearrange("p (s n) -> p s n", n=N)
                inv = iap[:, 1:N + 1].unsqueeze(1).broadcast_to([P, SEQ, N])
                dve.wait_ge(s_m["ek"], i + 1)
                dve.wait_ge(s_m["kvr"], 3 * i + 2)
                m.link(nc.vector.tensor_tensor(ekv[:, :], ek[:, :], bank[2][:, :], ALU.mult))
                m.mark(nc.vector.tensor_tensor(v3(fab[:, 0, :]), v3(ekv[:, :]), inv, ALU.mult))
                dve.wait_ge(s_m["sum"], i + 1)
                m.link(nc.vector.tensor_tensor(v3(fab[:, 1, :]), v3(bank[4][:, :]), inv, ALU.mult))
                wait(dve, s_m["st"], 2 * i)
                for k in range(2):
                    for s in range(SEQ):
                        last = nc.vector.tensor_tensor_scan(cs[:, k, s, 1:N + 1], onesn[:, :],
                                                            fab[:, k, s * N:(s + 1) * N], 0.0, ALU.mult, ALU.add)
                    last.then_inc(s_m["cs"], 1)
                for k in range(2):
                    dve.wait_ge(s_m["st"], 2 * i + k + 1)
                    m.link(nc.vector.tensor_scalar(scl[:, k, :], sraw[:, k, :], -FMAX, FMAX, ALU.max, ALU.min))
                    m.link(nc.vector.scalar_tensor_tensor(sst[:, k, :], sraw[:, k, :], FMAX, scl[:, k, :],
                                                          ALU.is_le, ALU.mult))
                m.mark(nc.vector.scalar_tensor_tensor(num[:, :], ekv[:, :], nlw[:, 1:2], sst[:, 0, :], ALU.mult, ALU.add))
                m.link(nc.vector.scalar_tensor_tensor(den[:, :], bank[4][:, :], nlw[:, 1:2], sst[:, 1, :],
                                                      ALU.mult, ALU.add))
                m.link(nc.vector.tensor_scalar(dmx[:, :], den[:, :], 1e-6, None, ALU.max))
                dve.wait_ge(s_m["er"], i + 1)
                m.link(nc.vector.scalar_tensor_tensor(rec[:, :], er[:, :], 1.0, dmx[:, :], ALU.add, ALU.mult))
                m.link(nc.vector.reciprocal(den[:, :], rec[:, :]))
                nc.vector.tensor_tensor(oT[:, :], num[:, :], den[:, :], ALU.mult).then_inc(s_m["o"], 1)
                assert m.count == per
                dve.wait_ge(s_m["y"], i + 1)
                xc = X[:, bass.ds(CT * i, CT), :].rearrange("p t c -> p (t c)")
                nc.vector.tensor_tensor(xc, xc, bank[5][:, :], ALU.add).then_inc(s_m["res"], 1)

            dve.wait_ge(s_m["res"], CH)
            dve_stats(chain, base + LS + 2)
            dve_rstd(chain, 3)
            dve.wait_ge(s_w3, 16 * 4)
            f = Chain(dve, s_f["ch"])
            per3 = 5
            @over_chunks(dve)
            def _(i):
                f.at(per3 * i)
                dve_norm(i, 0, s_f["xn"])
                dve.wait_ge(s_f["lg"], i + 1)
                f.link(nc.vector.tensor_tensor(lg[:, :, :], bank[1][:, 0:CT * E].rearrange("p (t e) -> p t e", e=E),
                                               brb[:, :].unsqueeze(1).broadcast_to([P, CT, E]), ALU.add))
                f.link(nc.vector.tensor_reduce(mx[:, :], lg[:, :, :], AX.X, ALU.max))
                f.link(nc.vector.tensor_tensor(eq[:, :, :], lg[:, :, :], mx[:, :].unsqueeze(2).broadcast_to([P, CT, E]),
                                               ALU.is_equal))
                f.link(nc.vector.tensor_tensor(wt[:, :, :], eq[:, :, :], desc[:, :].unsqueeze(1).broadcast_to([P, CT, E]),
                                               ALU.mult))
                f.link(nc.vector.tensor_reduce(mx[:, :], wt[:, :, :], AX.X, ALU.max))
                nc.vector.tensor_tensor(eq[:, :, :], wt[:, :, :], mx[:, :].unsqueeze(2).broadcast_to([P, CT, E]),
                                        ALU.is_equal).then_inc(s_f["eq"], 1)
                dve.wait_ge(s_f["eq"], i + 1)
                for e in range(E):
                    dve.wait_ge(s_f["y"], E * i + e + 1)
                    wait(dve, s_f["acc"], E * i + e)
                    for t in range(CT):
                        xc = X[:, bass.ds(CT * i + t, 1), :].rearrange("p o c -> p (o c)")
                        last = nc.vector.scalar_tensor_tensor(xc, bank[6 + e % 2][:, t * P:(t + 1) * P],
                                                              eq[:, t, e:e + 1], xc, ALU.mult, ALU.add)
                    last.then_inc(s_f["acc"], 1)


_INS = ['x', 'ctx_768', 'L0_xattn_Wq', 'L0_xattn_Wk', 'L0_xattn_Wv', 'L0_xattn_Wo', 'L0_xattn_bo',
        'L0_attn_mix_k', 'L0_attn_mix_v', 'L0_attn_mix_r', 'L0_attn_W_key', 'L0_attn_W_value',
        'L0_attn_W_receptance', 'L0_attn_W_output', 'L0_attn_time_decay', 'L0_attn_time_first',
        'L0_ffn_Wr', 'L0_ffn_br', 'L0_ffn_W1', 'L0_ffn_b1', 'L0_ffn_W2', 'L0_ffn_b2']
_OUTS = [((128, 32, 128), 'float32')]


def kernel(**inputs):
    import numpy as _np
    import concourse.bacc as _bacc
    from concourse import mybir as _mybir
    from concourse.bass_utils import run_bass_kernel_spmd as _run

    nc = _bacc.Bacc("TRN2", target_bir_lowering=False, num_devices=1)
    arrays, args = {}, []
    for name in _INS:
        a = _np.ascontiguousarray(inputs[name])
        arrays[f"in_{name}_dram"] = a
        args.append(nc.dram_tensor(f"in_{name}_dram", a.shape, _mybir.dt.from_np(a.dtype), kind="ExternalInput").ap())
    for i, (shape, dtype) in enumerate(_OUTS):
        dt = _mybir.dt.from_np(_np.dtype(dtype))
        args.append(nc.dram_tensor(f"out_{i}_dram", shape, dt, kind="ExternalOutput").ap())
    perceiver_layer_kernel(nc, *args)
    r = _run(nc, [arrays], core_ids=[0])
    return r.results[0]["out_0_dram"]
```

```python
from contextlib import ExitStack

import concourse.bass as bass
from concourse import mybir

ALU = mybir.AluOpType
ACT = mybir.ActivationFunctionType
AX = mybir.AxisListType
F32 = mybir.dt.float32
F16 = mybir.dt.float16

P = 128
EPS = 1e-5
FMAX = 3.4028234663852886e38


def wait(eng, sem, value):
    if isinstance(value, int) and value <= 0:
        return
    eng.wait_ge(sem, value)


class Chain:

    def __init__(self, eng, sem):
        self.eng, self.sem, self.base, self.count = eng, sem, 0, 0

    def at(self, base):
        self.base, self.count = base, 0

    def link(self, ins):
        self.count += 1
        ins.then_inc(self.sem, 1)
        self.eng.wait_ge(self.sem, self.base + self.count)

    def mark(self, ins):
        self.count += 1
        ins.then_inc(self.sem, 1)


def perceiver_layer_kernel(nc, x, ctx, Wq, Wk, Wv, Wo, bo, mix_k, mix_v, mix_r, W_key, W_value,
                           W_rec, W_out, decay, first, Wr, br, W1, b1, W2, b2, out):
    B, N, C = x.shape
    _, M, CC = ctx.shape
    HD = Wq.shape[1]
    H = 16
    D = HD // H
    SCALE = float(D) ** -0.5
    TOK = B * N
    G = TOK // P
    GB = P // N
    QT = H * N // P
    Q = H * N
    MC = M // P
    LAST = M - 1
    assert M == MC * P + 1 and Q == 512
    NP2 = 2
    CH = 8
    CT = G // CH
    SEQ = CT * GB
    T = CT * P
    E = Wr.shape[0]
    FF = W1.shape[1]
    FC = FF // P
    HS = C // H
    R3 = 3
    LR = R3 * QT

    top = ExitStack()

    def sb(name, shape, dt=F32):
        return top.enter_context(nc.sbuf_tensor(name, shape, dt))

    def sem(name):
        return top.enter_context(nc.semaphore(name))

    with top:
        bank = [top.enter_context(nc.psum_tensor(f"bank{i}", [P, 512], F32)) for i in range(8)]

        X = sb("X", [P, G, C])
        identf = sb("identf", [P, P])
        one = sb("one", [P, 1])
        ident = sb("ident", [P, P], F16)
        stats = sb("stats", [P, G, 6])
        mean = sb("mean", [P, G])
        std = sb("std", [P, G])
        rst = sb("rst", [P, G])
        tmpv = sb("tmpv", [P, G])
        varp = sb("varp", [P, G])
        xn = sb("xn", [P, 2, CT, C])

        s_id = sem("s_id")
        s_const = sem("s_const")
        s_x = sem("s_x")
        s_stat = sem("s_stat")
        s_var = sem("s_var")
        s_std = sem("s_std")
        s_ln = sem("s_ln")
        s_out = sem("s_out")

        s_w = sem("s_w")
        s_wT = sem("s_wT")
        s_wTc = sem("s_wTc")
        s_ab = sem("s_ab")
        s_abh = sem("s_abh")
        s_abl = sem("s_abl")
        s_xn1 = sem("s_xn1")
        s_x1T = sem("s_x1T")
        s_x1h = sem("s_x1h")
        s_x1l = sem("s_x1l")
        s_bo = sem("s_bo")
        s_raw0 = sem("s_raw0")
        s_p1end = sem("s_p1end")
        s_ctx = [sem(f"s_ctx{i}") for i in range(NP2)]
        s_chi = sem("s_chi")
        s_clo = sem("s_clo")
        s_c256 = sem("s_c256")
        s_ch = sem("s_ch")
        s_zd = sem("s_zd")
        s_z = [sem(f"s_z{i}") for i in range(NP2)]
        s_ctxT = sem("s_ctxT")
        s_cT = sem("s_cT")
        s_q = sem("s_q")
        s_qh = sem("s_qh")
        s_ql = sem("s_ql")
        s_S = sem("s_S")
        s_nmax = sem("s_nmax")
        s_exp = sem("s_exp")
        s_rs = sem("s_rs")
        s_pn = sem("s_pn")
        s_ehi = sem("s_ehi")
        s_elo = sem("s_elo")
        s_left = sem("s_left")
        s_L12 = sem("s_L12")
        s_T = sem("s_T")
        s_Th = sem("s_Th")
        s_Tl = sem("s_Tl")
        s_PV = sem("s_PV")
        s_Oh = sem("s_Oh")
        s_Ol = sem("s_Ol")
        s_y = sem("s_y")
        s_res = sem("s_res")
        s_w2 = sem("s_w2")
        s_w2T = sem("s_w2T")
        s_w2Tc = sem("s_w2Tc")
        s_tab = sem("s_tab")
        s_texp = sem("s_texp")
        s_tdve = sem("s_tdve")
        s_ln2 = sem("s_ln2")
        s_m = {n: sem("m_" + n) for n in ("xn", "xT", "xc", "tmp", "mix", "kvr", "ek", "er", "er1", "sum",
                                          "cs", "st", "o", "y", "res", "ch")}
        s_w3 = sem("s_w3")
        s_w3e = [sem(f"s_w3e{i}") for i in range(2)]
        s_w3T = sem("s_w3T")
        s_w3Tc = sem("s_w3Tc")
        s_f = {n: sem("f_" + n) for n in ("xn", "xT", "xc", "lg", "h", "hr", "y", "acc", "ch", "eq")}

        block = top.enter_context(nc.Block())

        arena = ExitStack()

        def asb(name, shape, dt=F32):
            return arena.enter_context(nc.sbuf_tensor(name, shape, dt))

        x1h = asb("x1h", [P, TOK], F16)
        x1l = asb("x1l", [P, TOK], F16)
        bob = asb("bob", [P, C])
        Ahi = asb("Ahi", [P, H, CC], F16)
        Alo = asb("Alo", [P, H, CC], F16)
        Bhi = asb("Bhi", [CC, H, C], F16)
        Blo = asb("Blo", [CC, H, C], F16)
        raw = asb("raw", [P, NP2, GB, MC + 1, CC])
        NC8 = NP2 * GB
        chi = asb("chi", [P, NC8, MC + 1, CC], F16)
        clo = asb("clo", [P, NC8, MC + 1, CC], F16)
        c256 = asb("c256", [P, CC])
        c256h = asb("c256h", [P, CC], F16)
        c256l = asb("c256l", [P, CC], F16)
        Z = asb("Z", [LR, NP2, GB, QT, CC], F16)
        MP = M + 1
        cT = asb("cT", [CC, 4, 2, MP], F16)
        qh = asb("qh", [CC, NP2, GB, Q], F16)
        ql = asb("ql", [CC, NP2, GB, Q], F16)
        nmax = asb("nmax", [P, NP2, QT])
        sums = asb("sums", [P, NP2, QT])
        rsum = asb("rsum", [P, NP2, QT])
        Pe = asb("Pe", [P, NP2, QT, M])
        Pn = asb("Pn", [P, NP2, QT, M])
        e12 = asb("e12", [P, NP2, R3, QT], F16)
        Th = asb("Th", [P, NP2, MC, Q], F16)
        Tl = asb("Tl", [P, NP2, MC, Q], F16)
        L12 = asb("L12", [LR, NP2, P], F16)
        Oh = asb("Oh", [CC, NP2, H, P], F16)
        Ol = asb("Ol", [CC, NP2, H, P], F16)
        warena = ExitStack()
        wq_r = warena.enter_context(nc.sbuf_tensor("wq_r", [P, HD], F32))
        wk_r = warena.enter_context(nc.sbuf_tensor("wk_r", [CC, HD], F32))
        wv_r = warena.enter_context(nc.sbuf_tensor("wv_r", [CC, HD], F32))
        wo_r = warena.enter_context(nc.sbuf_tensor("wo_r", [P, H // 2, C], F32))
        wqT = warena.enter_context(nc.sbuf_tensor("wqT", [P, H // 2, P], F32))
        wkT = warena.enter_context(nc.sbuf_tensor("wkT", [P, H // 2, CC], F32))
        wvT = warena.enter_context(nc.sbuf_tensor("wvT", [P, H // 2, CC], F32))
        warena.close()
        arena.close()

        late = ExitStack()

        def lsb(name, shape, dt=F32):
            return late.enter_context(nc.sbuf_tensor(name, shape, dt))

        w2r = lsb("w2r", [P, 4, C])
        w2T = lsb("w2T", [P, 4, C])
        mix = lsb("mix", [P, 3])
        omm = lsb("omm", [P, 3])
        dcy = lsb("dcy", [P, 2])
        nlw = lsb("nlw", [P, 2])
        nlw2 = lsb("nlw2", [P, 2])
        tt = lsb("tt", [P, N + 1])
        apw = lsb("apw", [P, N + 1])
        iap = lsb("iap", [P, N + 1])
        blk = lsb("blk", [P, P])
        onesn = lsb("onesn", [P, N])
        xT33 = lsb("xT33", [P, SEQ, N + 1])
        tmp3 = lsb("tmp3", [P, 3, T])
        xm3 = lsb("xm3", [P, 3, T])
        ek = lsb("ek", [P, T])
        er = lsb("er", [P, T])
        dmx = lsb("dmx", [P, T])
        ekv = lsb("ekv", [P, T])
        fab = lsb("fab", [P, 2, T])
        cs = lsb("cs", [P, 2, SEQ, N + 1])
        sraw = lsb("sraw", [P, 2, T])
        scl = lsb("scl", [P, 2, T])
        sst = lsb("sst", [P, 2, T])
        num = lsb("num", [P, T])
        den = lsb("den", [P, T])
        rec = lsb("rec", [P, T])
        oT = lsb("oT", [P, T])
        w1r = lsb("w1r", [P, 2, FC, C])
        w2fr = lsb("w2fr", [P, 2, FF])
        W1T = lsb("W1T", [P, E, FF])
        W2T = lsb("W2T", [P, E, FC, C])
        wrr = lsb("wrr", [E, C])
        wrT = lsb("wrT", [P, E])
        brb = lsb("brb", [P, E])
        b1r = lsb("b1r", [E * FC, P])
        b1T = lsb("b1T", [P, E * FC])
        b2r = lsb("b2r", [1, E * C])
        ones1 = lsb("ones1", [1, P])
        desc = lsb("desc", [P, E])
        x3T = lsb("x3T", [P, T])
        lg = lsb("lg", [P, CT, E])
        eq = lsb("eq", [P, CT, E])
        wt = lsb("wt", [P, CT, E])
        mx = lsb("mx", [P, CT])
        hb = lsb("hb", [P, 2, FC, T])
        late.close()

        bankh = [b[:, :].bitcast(F16) for b in bank]

        zdram = nc.dram_tensor("last_rows", [R3, B, CC], F16, kind="Internal").ap()
        SB = (0, 1, 2, 0)
        xt_dram = x.rearrange("(g b) n c -> (b n) g c", b=GB)
        out_dram = out.rearrange("(g b) n c -> (b n) g c", b=GB)
        ctx_main = ctx[:, 0:MC * P, :].rearrange("b (p s) c -> p b s c", s=MC)
        col = lambda a: a.rearrange("a b c -> c (a b)")

        def heads(buf, k):
            return buf[:, :, :].rearrange("p (q two) c -> p two q c", two=2)[:, k % 2, 4 * (k // 2):4 * (k // 2) + 4, :]


        def where(it, j):
            return 8 * it + j, 2 * it + j // GB, j % GB, (j // GB) % NP2

        def pe_ctxT(n, s8, s4):
            wait(nc.tensor, s_clo, n + 1)
            wait(nc.tensor, s_cT, n)
            wait(nc.tensor, s_L12, n - 2)
            for half, src in enumerate((chi, clo)):
                for c in range(MC):
                    nc.tensor.transpose(bankh[7][0:CC, half * MP + c * P:half * MP + (c + 1) * P],
                                        src[:, s8, c, :], ident[:, :])
                last = nc.tensor.transpose(bankh[7][0:CC, half * MP + MC * P:half * MP + MC * P + 2],
                                           src[0:2, s8, MC, :], ident[0:2, 0:2])
            last.then_inc(s_ctxT, 1)

        def pe_scores(n, par, b, s4, tiles):
            wait(nc.tensor, s_cT, n + 1)
            for t in tiles:
                wait(nc.tensor, s_exp, QT * n + 1 if t == 3 else QT * (n - 1) + (t or 3) + 1)
                for k, (w, c) in enumerate(((qh, 0), (qh, 1), (ql, 0))):
                    last = nc.tensor.matmul(bank[SB[t]][:, 0:M], w[:, par, b, t * P:(t + 1) * P],
                                            cT[:, s4, c, 0:M], start=(k == 0), stop=(k == 2))
                last.then_inc(s_S, 1)

        def pe_q(k, c, tok):
            wait(nc.tensor, s_ql, k)
            for hh in range(QT):
                h = QT * c + hh
                for k, (w, a) in enumerate(((Ahi, x1h), (Ahi, x1l), (Alo, x1h))):
                    last = nc.tensor.matmul(bank[3][0:CC, hh * P:(hh + 1) * P], w[:, h, :], a[:, tok],
                                            start=(k == 0), stop=(k == 2))
            last.then_inc(s_q, 1)

        def pe_pv(n, par, s8, gp, b, pairs):
            wait(nc.tensor, s_Ol, n)
            k = 0
            for w, p, s in ((chi, Th, s_Th), (clo, Th, None), (chi, Tl, s_Tl)):
                for c in range(MC):
                    if s is not None:
                        wait(nc.tensor, s, MC * n + c + 1)
                    nc.tensor.matmul(bank[6][0:CC, :], w[:, s8, c, :], p[:, par, c, :], start=(k == 0), stop=False)
                    k += 1
            wait(nc.tensor, s_L12, n + 1)
            if b == 0:
                wait(nc.tensor, s_z[gp], 16 * QT * pairs)
            for t in range(QT):
                last = nc.tensor.matmul(bank[6][0:CC, t * P:(t + 1) * P], Z[:, gp, b, t, :], L12[:, par, :],
                                        start=False, stop=(t == QT - 1))
            last.then_inc(s_PV, 1)

        def pe_y(g, gp):
            wait(nc.tensor, s_Ol, GB * (g + 1))
            for h in range(H):
                for k, (o, w) in enumerate(((Oh, Bhi), (Oh, Blo), (Ol, Bhi))):
                    last = nc.tensor.matmul(bank[3][:, 0:C], o[:, gp, h, :], w[:, h, :],
                                            start=(h == 0 and k == 0), stop=(h == H - 1 and k == 2))
            last.then_inc(s_y, 1)

        def pe_probsT(n, par):
            for c in range(MC):
                wait(nc.tensor, s_Tl, MC * (n - 1) + c + 1)
                for t in range(QT):
                    last = nc.tensor.transpose(bank[4 + c][:, t * P:(t + 1) * P], Pn[:, par, t, c * P:(c + 1) * P],
                                               identf[:, :])
                last.then_inc(s_T, 1)

        def exists(n, last=B):
            return not isinstance(n, int) or 0 <= n < last

        def pe_step(it, j):
            n, g, jj, gp = where(it, j)
            if exists(n + 2):
                pe_ctxT(n + 2, (j + 2) % NC8, (j + 2) % 4)
            if exists(n + 1):
                if (j + 1) % GB == 0:
                    wait(nc.tensor, s_ql, n + 5)
                pe_scores(n + 1, ((j + 1) // GB) % NP2, (j + 1) % GB, (j + 1) % 4, (0, 1, 2))
            if exists(n + 5):
                if (j + 1) % GB == GB - 1:
                    wait(nc.tensor, s_res, g)
                pe_q(n + 5, (j + 1) % GB, bass.ds(P * (g + 1 + (jj + 1) // GB), P))
            if exists(n + 1):
                pe_scores(n + 1, ((j + 1) // GB) % NP2, (j + 1) % GB, (j + 1) % 4, (3,))
            if exists(n - 1):
                pe_pv(n - 1, (j - 1) % NP2, (j - 1) % NC8, ((j - 1) // GB) % NP2, (j - 1) % GB,
                      it + 1 + (j - 1) // NC8)
            if jj == 1 and exists(g - 1, G):
                if exists(n + 5):
                    wait(nc.tensor, s_ql, n + 6)
                pe_y(g - 1, 1 - gp)
            if exists(n):
                if exists(n + 2):
                    wait(nc.tensor, s_cT, n + 3)
                else:
                    wait(nc.tensor, s_L12, n)
                wait(nc.tensor, s_elo, n + 1)
                nc.tensor.transpose(bankh[7][0:LR, 0:P], e12[:, n_par(j), :, :].rearrange("p r t -> p (r t)"),
                                    ident[:, :]).then_inc(s_left, 1)
                wait(nc.tensor, s_pn, n + 1)
                pe_probsT(n, n_par(j))

        def n_par(j):
            return j % NP2

        def act_step(it, j):
            n, g, jj, gp = where(it, j)
            if exists(n - 1):
                wait(nc.scalar, s_PV, n - 2)
                for c in range(MC):
                    wait(nc.scalar, s_T, MC * (n - 1) + c + 1)
                    nc.scalar.activation(Th[:, n_par(j - 1), c, :], bank[4 + c][:, :], ACT.Copy).then_inc(s_Th, 1)
            for t in range(QT):
                if exists(n + 1):
                    if t == 0:
                        wait(nc.scalar, s_elo, n)
                    wait(nc.scalar, s_nmax, QT * (n + 1) + t + 1)
                    nc.scalar.activation(Pe[:, n_par(j + 1), t, :], bank[SB[t]][:, 0:M], ACT.Exp,
                                         bias=nmax[:, n_par(j + 1), t:t + 1],
                                         accum_out=sums[:, n_par(j + 1), t:t + 1]).then_inc(s_exp, 1)
                if t == 2 and exists(n + 5):
                    act_q(n + 5, (gp + 1 + (jj + 1) // GB) % NP2, (j + 1) % GB)
            if exists(n - 1):
                if (j - 1) % GB == 0:
                    wait(nc.scalar, s_y, g - 1)
                wait(nc.scalar, s_PV, n)
                nc.scalar.activation(Oh[:, ((j - 1) // GB) % NP2, :, ((j - 1) % GB) * N:((j - 1) % GB + 1) * N],
                                     bank[6][0:CC, :].rearrange("p (h t) -> p h t", h=H), ACT.Copy).then_inc(s_Oh, 1)

        def q_view(buf, par, c):
            return buf[:, par, :, c * P:(c + 1) * P].rearrange("p b (h t) -> p h b t", h=QT)

        def act_q(k, par, c):
            wait(nc.scalar, s_q, k + 1)
            wait(nc.scalar, s_S, QT * (k - c) - QT * GB)
            nc.scalar.activation(q_view(qh, par, c), bank[3][0:CC, :].rearrange("p (h b t) -> p h b t", h=QT, b=GB),
                                 ACT.Copy).then_inc(s_qh, 1)

        def dve_q(k, par, c):
            wait(nc.vector, s_qh, k + 1)
            nc.vector.tensor_tensor(q_view(ql, par, c), bank[3][0:CC, :].rearrange("p (h b t) -> p h b t", h=QT, b=GB),
                                    q_view(qh, par, c), ALU.subtract).then_inc(s_ql, 1)

        def dve_step(it, j):
            n, g, jj, gp = where(it, j)
            if exists(n + 2):
                dve_cT(n + 2, (j + 2) % 4)
            for kind, t in (("max", 0), ("max", 1), ("low", 0), ("max", 2), ("low", 1), ("max", 3)):
                if kind == "low" and exists(n - 1):
                    wait(nc.vector, s_Th, MC * (n - 1) + t + 1)
                    nc.vector.tensor_tensor(Tl[:, n_par(j - 1), t, :], bank[4 + t][:, :], Th[:, n_par(j - 1), t, :],
                                            ALU.subtract).then_inc(s_Tl, 1)
                if kind == "max" and exists(n + 1):
                    wait(nc.vector, s_S, QT * (n + 1) + t + 1)
                    nc.vector.tensor_reduce(nmax[:, n_par(j + 1), t:t + 1], bank[SB[t]][:, 0:M], AX.X, ALU.max,
                                            negate=True).then_inc(s_nmax, 1)
            if exists(n + 5):
                dve_q(n + 5, (gp + 1 + (jj + 1) // GB) % NP2, (j + 1) % GB)
            if exists(n + 1):
                wait(nc.vector, s_exp, QT * (n + 2))
                wait(nc.vector, s_pn, n)
                nc.vector.reciprocal(rsum[:, n_par(j + 1), :], sums[:, n_par(j + 1), :]).then_inc(s_rs, 1)
            if exists(n):
                wait(nc.vector, s_left, n + 1)
                wait(nc.vector, s_PV, n - 1)
                nc.vector.tensor_copy(L12[:, n_par(j), :], bankh[7][0:LR, 0:P]).then_inc(s_L12, 1)
            if exists(n - 1):
                wait(nc.vector, s_Oh, n)
                sl = (slice(None), ((j - 1) // GB) % NP2, slice(None), slice(((j - 1) % GB) * N, ((j - 1) % GB + 1) * N))
                nc.vector.tensor_tensor(Ol[sl], bank[6][0:CC, :].rearrange("p (h t) -> p h t", h=H), Oh[sl],
                                        ALU.subtract).then_inc(s_Ol, 1)
            if jj == 1 and exists(g - 1, G):
                wait(nc.vector, s_y, g)
                tile = X[:, bass.ds(g - 1, 1), :].rearrange("p o c -> p (o c)")
                nc.vector.tensor_tensor(tile, tile, bank[3][:, 0:C], ALU.add).then_inc(s_res, 1)

        def dve_cT(n, s4):
            wait(nc.vector, s_ctxT, n + 1)
            nc.vector.tensor_copy(cT[:, s4, :, :].rearrange("p s m -> p (s m)"), bankh[7][0:CC, 0:2 * MP])\
                .then_inc(s_cT, 1)

        def pool_prep(n, s8, par, b):
            wait(nc.gpsimd, s_PV, n - 7)
            nc.gpsimd.tensor_tensor(chi[:, s8, :, :], raw[:, par, b, :, :],
                                    one[:, 0:1].unsqueeze(2).broadcast_to([P, MC + 1, CC]), ALU.mult)\
                .then_inc(s_chi, 1)
            wait(nc.gpsimd, s_chi, n + 1)
            nc.gpsimd.tensor_tensor(clo[:, s8, :, :], raw[:, par, b, :, :], chi[:, s8, :, :], ALU.subtract)\
                .then_inc(s_clo, 1)

        def pool_step(it, j):
            n, g, jj, gp = where(it, j)
            if exists(n + 1):
                wait(nc.gpsimd, s_rs, n + 2)
                wait(nc.gpsimd, s_T, MC * n)
                par = n_par(j + 1)
                nc.gpsimd.tensor_tensor(Pn[:, par, :, :], Pe[:, par, :, :],
                                        rsum[:, par, :].unsqueeze(2).broadcast_to([P, QT, M]), ALU.mult)\
                    .then_inc(s_pn, 1)
                wait(nc.gpsimd, s_pn, n + 2)
                wait(nc.gpsimd, s_left, n)
                lastcol = Pn[:, par, :, LAST:M].rearrange("p t o -> p (t o)")
                nc.gpsimd.tensor_tensor(e12[:, par, 0:R3:2, :], lastcol.unsqueeze(1).broadcast_to([P, 2, QT]),
                                        one[:, 0:1].unsqueeze(2).broadcast_to([P, 2, QT]), ALU.mult).then_inc(s_ehi, 1)
                wait(nc.gpsimd, s_ehi, n + 2)
                nc.gpsimd.tensor_tensor(e12[:, par, 1, :], lastcol, e12[:, par, 0, :], ALU.subtract).then_inc(s_elo, 1)
            if exists(n + 4):
                if (j + 4) % GB == 0:
                    wait(nc.gpsimd, s_ctx[((j + 4) // GB) % NP2], 32 * (it + 1 + ((j + 4) // GB - ((j + 4) // GB) % NP2) // NP2))
                pool_prep(n + 4, (j + 4) % NC8, ((j + 4) // GB) % NP2, (j + 4) % GB)

        def pipeline(eng, step):
            for j in range(-1, 7):
                step(0, j)
            with eng.Fori(1, B // 8 - 1) as it:
                for j in range(-1, 7):
                    step(it, j)
            for j in range(-1, 10):
                step(B // 8 - 1, j)

        def over_chunks(eng):
            def run(body):
                body(0)
                with eng.Fori(1, CH) as i:
                    body(i)
            return run

        LS = G + 6 + 5

        def dve_stats(chain, base):
            @over_chunks(nc.vector)
            def _(i):
                for t in range(CT):
                    nc.vector.bn_stats(stats[:, bass.ds(CT * i + t, 1), :].rearrange("p o s -> p (o s)"),
                                       X[:, bass.ds(CT * i + t, 1), :].rearrange("p o c -> p (o c)"))\
                        .then_inc(chain.sem, 1)
            chain.at(base + G)
            nc.vector.wait_ge(chain.sem, base + G)
            chain.mark(nc.vector.tensor_tensor(tmpv[:, :], stats[:, :, 1], stats[:, :, 4], ALU.add))
            chain.mark(nc.vector.tensor_tensor(std[:, :], stats[:, :, 1], stats[:, :, 4], ALU.subtract))
            chain.link(nc.vector.tensor_tensor(rst[:, :], stats[:, :, 2], stats[:, :, 5], ALU.add))
            chain.mark(nc.vector.tensor_scalar(mean[:, :], tmpv[:, :], 0.5, None, ALU.mult))
            chain.link(nc.vector.scalar_tensor_tensor(varp[:, :], std[:, :], 0.25, std[:, :], ALU.mult, ALU.mult))
            chain.link(nc.vector.tensor_scalar(tmpv[:, :], rst[:, :], 1.0 / C, EPS, ALU.mult, ALU.add))

        def dve_rstd(chain, phase):
            nc.vector.tensor_tensor(varp[:, :], varp[:, :], tmpv[:, :], ALU.add).then_inc(s_var, 1)
            nc.vector.wait_ge(s_var, phase)
            nc.vector.wait_ge(s_std, phase)
            chain.link(nc.vector.reciprocal(rst[:, :], std[:, :]))
            chain.link(nc.vector.tensor_tensor(tmpv[:, :], rst[:, :], rst[:, :], ALU.mult))
            chain.link(nc.vector.tensor_tensor(tmpv[:, :], tmpv[:, :], varp[:, :], ALU.mult))
            chain.link(nc.vector.tensor_scalar(tmpv[:, :], tmpv[:, :], -0.5, 1.5, ALU.mult, ALU.add))
            chain.link(nc.vector.tensor_tensor(rst[:, :], rst[:, :], tmpv[:, :], ALU.mult))

        def act_std(phase):
            nc.scalar.wait_ge(s_var, phase)
            nc.scalar.activation(std[:, :], varp[:, :], ACT.Sqrt).then_inc(s_std, 1)

        def dve_norm(i, par, s):
            for t in range(CT):
                k = CT * i + t
                last = nc.vector.tensor_scalar(xn[:, par, t, :], X[:, bass.ds(k, 1), :].rearrange("p o c -> p (o c)"),
                                               mean[:, bass.ds(k, 1)],
                                               rst[:, bass.ds(k, 1)], ALU.subtract, ALU.mult)
            last.then_inc(s, 1)

        def pe_norm_T(par, b, s):
            for t in range(CT):
                last = nc.tensor.transpose(bank[b][:, t * P:(t + 1) * P], xn[:, par, t, :], identf[:, :])
            last.then_inc(s, 1)

        @block.sync
        def _(sp):
            sp.dma_start(X[:, :, :], xt_dram).then_inc(s_x, 16)
            sp.dma_start(wq_r[:, :], Wq).then_inc(s_w, 16)
            sp.dma_start(wk_r[:, :], Wk).then_inc(s_w, 16)
            sp.dma_start(wv_r[:, :], Wv).then_inc(s_w, 16)
            sp.dma_start(wo_r[:, :, :], Wo.rearrange("(a p) c -> p a c", p=P)).then_inc(s_w, 16)
            sp.dma_start(bob[:, :], bo.rearrange("(o c) -> o c", o=1).broadcast_to([P, C])).then_inc(s_bo, 16)
            sp.dma_start(c256[:, :], ctx[:, LAST, :]).then_inc(s_c256, 16)
            sp.wait_ge(s_raw0, 2)

            def load_ctx(g, par):
                b0 = GB * g
                wait(sp, s_clo, GB * (g - 1))
                sp.dma_start(raw[:, par, :, 0:MC, :], ctx_main[:, bass.ds(b0, GB), :, :]).then_inc(s_ctx[par], 16)
                sp.dma_start(raw[0:1, par, :, MC, :], ctx[bass.ds(b0, GB), LAST:M, :].rearrange("b o c -> o b c"))\
                    .then_inc(s_ctx[par], 16)

            def load_z(g, par):
                wait(sp, s_PV, GB * (g - 1))
                for t in range(QT):
                    sp.dma_start(Z[t:LR:QT, par, :, t, :], zdram[:, bass.ds(GB * g, GB), :]).then_inc(s_z[par], 16)

            load_ctx(0, 0)
            load_ctx(1, 1)
            sp.wait_ge(s_ch, 2)
            for r, part in enumerate((c256h, c256h, c256l)):
                sp.dma_start(zdram[r], part[:, :]).then_inc(s_zd, 16)
            sp.wait_ge(s_zd, 16 * R3)
            load_z(0, 0)
            load_z(1, 1)
            with sp.Fori(1, G // 2) as i:
                for par in range(NP2):
                    load_ctx(2 * i + par, par)
                    load_z(2 * i + par, par)
            sp.wait_ge(s_res, G)
            for i, w in enumerate((W_key, W_value, W_rec, W_out)):
                sp.dma_start(w2r[:, i, :], w).then_inc(s_w2, 16)
            for i, m in enumerate((mix_k, mix_v, mix_r)):
                sp.dma_start(mix[:, i:i + 1], col(m)).then_inc(s_w2, 16)
            for i, v in enumerate((decay, first)):
                for a in range(HS):
                    sp.dma_start(dcy[a:P:HS, i:i + 1], v.rearrange("(h o) -> h o", o=1)).then_inc(s_w2, 16)
            sp.dma_start(wrr[:, :], Wr).then_inc(s_w3, 16)
            sp.dma_start(brb[:, :], br.rearrange("(o e) -> o e", o=1).broadcast_to([P, E])).then_inc(s_w3, 16)
            sp.dma_start(b1r[:, :], b1.rearrange("e (f p) -> (e f) p", p=P)).then_inc(s_w3, 16)
            sp.dma_start(b2r[:, :], b2.rearrange("(o e) d -> o (e d)", o=1)).then_inc(s_w3, 16)
            for e in range(E):
                if e >= 2:
                    sp.wait_ge(s_w3T, 1 + 2 * (e - 1))
                sp.dma_start(w1r[:, e % 2, :, :], W1[e].rearrange("(f p) d -> p f d", p=P)).then_inc(s_w3e[e % 2], 16)
                sp.dma_start(w2fr[:, e % 2, :], W2[e]).then_inc(s_w3e[e % 2], 16)
            @over_chunks(sp)
            def _(i):
                sp.wait_ge(s_f["acc"], E * (i + 1))
                sp.dma_start(out_dram[:, bass.ds(CT * i, CT), :], X[:, bass.ds(CT * i, CT), :]).then_inc(s_out, 16)
            sp.wait_ge(s_out, 16 * CH)

        @block.gpsimd
        def _(pool):
            nc.gpsimd.memset(identf[:, :], 0.0).then_inc(s_id, 1)
            nc.gpsimd.memset(one[:, :], 1.0).then_inc(s_id, 1)
            nc.gpsimd.memset(raw[:, :, :, MC, :], 0.0).then_inc(s_raw0, 1)
            nc.gpsimd.memset(Z[:, :, :, :, :], 0.0).then_inc(s_raw0, 1)
            pool.wait_ge(s_id, 2)
            nc.gpsimd.affine_select(out=identf[:, :], in_=identf[:, :], compare_op=ALU.not_equal, fill=1.0,
                                    base=0, pattern=[[-1, P]], channel_multiplier=1).then_inc(s_const, 1)
            pool.wait_ge(s_const, 1)
            nc.gpsimd.tensor_copy(ident[:, :], identf[:, :]).then_inc(s_const, 1)
            pool.wait_ge(s_const, 2)
            pool.wait_ge(s_c256, 16)
            nc.gpsimd.tensor_copy(c256h[:, :], c256[:, :]).then_inc(s_ch, 1)
            pool.wait_ge(s_ch, 1)
            nc.gpsimd.tensor_tensor(c256l[:, :], c256[:, :], c256h[:, :], ALU.subtract).then_inc(s_ch, 1)
            pool.wait_ge(s_ctx[0], 32)
            for b in range(GB - 1):
                pool_prep(b, b, 0, b)
            pool.wait_ge(s_bo, 16)
            pool.wait_ge(s_xn1, CH)
            nc.gpsimd.tensor_tensor(X[:, :, :], X[:, :, :], bob[:, :].unsqueeze(1).broadcast_to([P, G, C]), ALU.add)\
                .then_inc(s_bo, 1)
            pipeline(nc.gpsimd, pool_step)

            pool.wait_ge(s_res, G)
            nc.gpsimd.iota(tt[:, :], pattern=[[1, N + 1]], base=0, channel_multiplier=0,
                           allow_small_or_imprecise_dtypes=True).then_inc(s_tab, 1)
            nc.gpsimd.iota(desc[:, :], pattern=[[-1, E]], base=E, channel_multiplier=0,
                           allow_small_or_imprecise_dtypes=True).then_inc(s_tab, 1)
            nc.gpsimd.memset(xT33[:, :, :], 0.0).then_inc(s_tab, 1)
            nc.gpsimd.memset(cs[:, :, :, :], 0.0).then_inc(s_tab, 1)
            nc.gpsimd.memset(ones1[:, :], 1.0).then_inc(s_tab, 1)
            nc.gpsimd.memset(onesn[:, :], 1.0).then_inc(s_tab, 1)
            nc.gpsimd.memset(blk[:, :], 1.0).then_inc(s_tab, 1)
            pool.wait_ge(s_tab, 7)
            bv = blk[:, :].rearrange("p (h a) -> p h a", a=HS)
            nc.gpsimd.affine_select(out=bv, in_=bv, compare_op=ALU.is_ge, fill=0.0, base=0,
                                    pattern=[[-HS, H], [0, HS]], channel_multiplier=1).then_inc(s_tab, 1)
            pool.wait_ge(s_tab, 8)
            nc.gpsimd.affine_select(out=bv, in_=bv, compare_op=ALU.is_ge, fill=0.0, base=HS - 1,
                                    pattern=[[HS, H], [0, HS]], channel_multiplier=-1).then_inc(s_tab, 1)
            @over_chunks(nc.gpsimd)
            def _(i):
                pool.wait_ge(s_tdve, 1)
                pool.wait_ge(s_m["xc"], i + 1)
                for k in range(3):
                    last = nc.gpsimd.tensor_tensor(tmp3[:, k, :].rearrange("p (s n) -> p s n", n=N), xT33[:, :, 0:N],
                                                   omm[:, k:k + 1].unsqueeze(2).broadcast_to([P, SEQ, N]), ALU.mult)
                last.then_inc(s_m["tmp"], 1)
                for k in range(2):
                    pool.wait_ge(s_m["cs"], 2 * i + k + 1)
                    nc.gpsimd.tensor_tensor(sraw[:, k, :].rearrange("p (s n) -> p s n", n=N), cs[:, k, :, 0:N],
                                            apw[:, 0:N].unsqueeze(1).broadcast_to([P, SEQ, N]), ALU.mult)\
                        .then_inc(s_m["st"], 1)

        @block.scalar
        def _(act):
            act_std(1)
            for k in range(6):
                act.wait_ge(s_wT, k + 1)
                dst, w = ((wqT, P), (wkT, CC), (wvT, CC))[k // 2]
                nc.scalar.activation(dst[:, 4 * (k % 2):4 * (k % 2) + 4, :],
                                     bank[k % 2][:, 0:4 * w].rearrange("p (a c) -> p a c", a=4), ACT.Copy)\
                    .then_inc(s_wTc, 1)
            for k in range(8):
                act.wait_ge(s_ab, k + 1)
                if k < 4:
                    nc.scalar.activation(heads(Ahi, k),
                                         bank[2 + k % 2][:, 0:4 * CC].rearrange("p (a c) -> p a c", a=4), ACT.Copy,
                                         scale=SCALE).then_inc(s_abh, 1)
                else:
                    nc.scalar.activation(heads(Bhi, k - 4),
                                         bank[2 + k % 2][0:CC, :].rearrange("p (a c) -> p a c", a=4), ACT.Copy)\
                        .then_inc(s_abh, 1)
            @over_chunks(act)
            def _(i):
                act.wait_ge(s_x1T, i + 1)
                nc.scalar.activation(x1h[:, bass.ds(T * i, T)], bank[4][:, :], ACT.Copy).then_inc(s_x1h, 1)
            for c in range(QT):
                act_q(c, 0, c)
            pipeline(nc.scalar, act_step)

            act_std(2)
            act.wait_ge(s_w2T, 1)
            nc.scalar.activation(w2T[:, :, :].rearrange("p a c -> p (a c)"), bank[1][:, :], ACT.Copy).then_inc(s_w2Tc, 1)
            act.wait_ge(s_w2, 16 * (7 + 2 * HS))
            nc.scalar.activation(nlw[:, :], dcy[:, :], ACT.Exp).then_inc(s_texp, 1)
            act.wait_ge(s_tdve, 1)
            act.wait_ge(s_tab, 1)
            nc.scalar.activation(apw[:, :], tt[:, :], ACT.Exp, scale=nlw2[:, 0:1])\
                .then_inc(s_texp, 1)
            @over_chunks(act)
            def _(i):
                act.wait_ge(s_m["xT"], i + 1)
                wait(act, s_m["mix"], i)
                nc.scalar.activation(xT33[:, :, 1:N + 1], bank[0][:, :].rearrange("p (s n) -> p s n", n=N), ACT.Copy)\
                    .then_inc(s_m["xc"], 1)
                act.wait_ge(s_m["kvr"], 3 * i + 1)
                wait(act, s_m["res"], i)
                nc.scalar.activation(ek[:, :], bank[1][:, :], ACT.Exp).then_inc(s_m["ek"], 1)
                act.wait_ge(s_m["kvr"], 3 * i + 3)
                nc.scalar.activation(er[:, :], bank[3][:, :], ACT.Exp, scale=-1.0).then_inc(s_m["er"], 1)

            act_std(3)
            act.wait_ge(s_w3T, 1)
            nc.scalar.activation(wrT[:, :], bank[0][:, 0:E], ACT.Copy).then_inc(s_w3Tc, 1)
            nc.scalar.activation(b1T[:, :], bank[0][:, E:E + E * FC], ACT.Copy).then_inc(s_w3Tc, 1)
            for e in range(E):
                act.wait_ge(s_w3T, 2 + 2 * e)
                nc.scalar.activation(W1T[:, e, :], bank[1][:, :], ACT.Copy).then_inc(s_w3Tc, 1)
                act.wait_ge(s_w3T, 3 + 2 * e)
                nc.scalar.activation(W2T[:, e, :, :].rearrange("p f c -> p (f c)"), bank[2][:, :], ACT.Copy)\
                    .then_inc(s_w3Tc, 1)
            act.wait_ge(s_w3Tc, 2 + 2 * E)
            @over_chunks(act)
            def _(i):
                act.wait_ge(s_f["xT"], i + 1)
                wait(act, s_f["y"], E * i)
                nc.scalar.activation(x3T[:, :], bank[0][:, :], ACT.Copy).then_inc(s_f["xc"], 1)
                for e in range(E):
                    if e >= 2:
                        act.wait_ge(s_f["y"], E * i + e - 1)
                    for f in range(FC):
                        act.wait_ge(s_f["h"], E * FC * i + FC * e + f + 1)
                        nc.scalar.activation(hb[:, e % 2, f, :], bank[2 + f][:, :], ACT.Relu,
                                             bias=b1T[:, FC * e + f:FC * e + f + 1]).then_inc(s_f["hr"], 1)

        @block.tensor
        def _(pe):
            pe.wait_ge(s_const, 2)
            pe.wait_ge(s_w, 16 * 4)
            for k in range(6):
                src, w = ((wq_r, P), (wk_r, CC), (wv_r, CC))[k // 2]
                wait(pe, s_wTc, k - 1)
                for a in range(4):
                    p = 4 * (k % 2) + a
                    last = nc.tensor.transpose(bank[k % 2][:, a * w:(a + 1) * w], src[:, p * P:(p + 1) * P],
                                               identf[0:w, 0:w])
                last.then_inc(s_wT, 1)
            pe.wait_ge(s_wTc, 6)
            for k in range(8):
                wait(pe, s_abl, k - 1)
                for a in range(4):
                    lo, pair = (k % 2) * D, (k % 4) // 2 * 4 + a
                    if k < 4:
                        last = nc.tensor.matmul(bank[2 + k % 2][:, a * CC:(a + 1) * CC], wqT[lo:lo + D, pair, :],
                                                wkT[lo:lo + D, pair, :], start=True, stop=True)
                    else:
                        last = nc.tensor.matmul(bank[2 + k % 2][0:CC, a * C:(a + 1) * C], wvT[lo:lo + D, pair, :],
                                                wo_r[lo:lo + D, pair, :], start=True, stop=True)
                last.then_inc(s_ab, 1)
            @over_chunks(pe)
            def _(i):
                pe.wait_ge(s_xn1, i + 1)
                wait(pe, s_x1l, i)
                pe_norm_T(0, 4, s_x1T)
            pe.wait_ge(s_x1l, CH)
            pe.wait_ge(s_abl, 8)
            pe_ctxT(0, 0, 0)
            for c in range(QT):
                pe_q(c, c, slice(0, P))
            pe.wait_ge(s_ql, QT)
            pipeline(nc.tensor, pe_step)

            pe.wait_ge(s_res, G)
            pe.wait_ge(s_w2, 16 * (7 + 2 * HS))
            for a in range(4):
                last = nc.tensor.transpose(bank[1][:, a * P:(a + 1) * P], w2r[:, a, :], identf[:, :])
            last.then_inc(s_w2T, 1)
            pe.wait_ge(s_w2Tc, 1)
            pe.wait_ge(s_tab, 9)
            @over_chunks(pe)
            def _(i):
                pe.wait_ge(s_m["xn"], i + 1)
                pe_norm_T(0, 0, s_m["xT"])
                for k in range(3):
                    pe.wait_ge(s_m["mix"], i + 1)
                    nc.tensor.matmul(bank[1 + k][:, :], w2T[:, k, :], xm3[:, k, :], start=True, stop=True)\
                        .then_inc(s_m["kvr"], 1)
                pe.wait_ge(s_m["ek"], i + 1)
                nc.tensor.matmul(bank[4][:, :], blk[:, :], ek[:, :], start=True, stop=True).then_inc(s_m["sum"], 1)
                pe.wait_ge(s_m["o"], i + 1)
                for t in range(CT):
                    last = nc.tensor.matmul(bank[5][:, t * P:(t + 1) * P], oT[:, t * P:(t + 1) * P], w2T[:, 3, :],
                                            start=True, stop=True)
                last.then_inc(s_m["y"], 1)

            pe.wait_ge(s_w3, 16 * 4)
            pe.wait_ge(s_m["res"], CH)
            nc.tensor.transpose(bank[0][:, 0:E], wrr[:, :], identf[0:E, 0:E])
            nc.tensor.transpose(bank[0][:, E:E + E * FC], b1r[:, :], identf[0:E * FC, 0:E * FC]).then_inc(s_w3T, 1)
            for e in range(E):
                pe.wait_ge(s_w3e[e % 2], 32 * (e // 2 + 1))
                wait(pe, s_w3Tc, 2 + 2 * e if e else 0)
                for f in range(FC):
                    last = nc.tensor.transpose(bank[1][:, f * P:(f + 1) * P], w1r[:, e % 2, f, :], identf[:, :])
                last.then_inc(s_w3T, 1)
                for f in range(FC):
                    last = nc.tensor.transpose(bank[2][:, f * P:(f + 1) * P], w2fr[:, e % 2, f * P:(f + 1) * P],
                                               identf[:, :])
                last.then_inc(s_w3T, 1)
            pe.wait_ge(s_w3Tc, 2 + 2 * E)
            @over_chunks(pe)
            def _(i):
                pe.wait_ge(s_f["xn"], i + 1)
                pe_norm_T(0, 0, s_f["xT"])
                pe.wait_ge(s_f["xc"], i + 1)
                for t in range(CT):
                    last = nc.tensor.matmul(bank[1][:, t * E:(t + 1) * E], x3T[:, t * P:(t + 1) * P], wrT[:, :],
                                            start=True, stop=True)
                last.then_inc(s_f["lg"], 1)
                for e in range(E + 1):
                    if e < E:
                        for f in range(FC):
                            if e:
                                pe.wait_ge(s_f["hr"], E * FC * i + FC * (e - 1) + f + 1)
                            nc.tensor.matmul(bank[2 + f][:, :], W1T[:, e, f * P:(f + 1) * P], x3T[:, :],
                                             start=True, stop=True).then_inc(s_f["h"], 1)
                    if e:
                        y = e - 1
                        pe.wait_ge(s_f["hr"], E * FC * i + FC * e)
                        if y >= 2:
                            pe.wait_ge(s_f["acc"], E * i + y - 1)
                        for t in range(CT):
                            o = bank[6 + y % 2][:, t * P:(t + 1) * P]
                            for f in range(FC):
                                nc.tensor.matmul(o, hb[:, y % 2, f, t * P:(t + 1) * P], W2T[:, y, f, :],
                                                 start=(f == 0), stop=False)
                            last = nc.tensor.matmul(o, ones1[:, :], b2r[:, y * C:(y + 1) * C], start=False, stop=True)
                        last.then_inc(s_f["y"], 1)

        @block.vector
        def _(dve):
            chain = Chain(dve, s_ln)
            dve.wait_ge(s_x, 16)
            dve_stats(chain, 0)
            dve_rstd(chain, 1)
            for k in range(8):
                dve.wait_ge(s_abh, k + 1)
                if k < 4:
                    nc.vector.scalar_tensor_tensor(heads(Alo, k), bank[2 + k % 2][:, 0:4 * CC].rearrange("p (a c) -> p a c", a=4),
                                                   SCALE, heads(Ahi, k), ALU.mult, ALU.subtract).then_inc(s_abl, 1)
                else:
                    nc.vector.tensor_tensor(heads(Blo, k - 4), bank[2 + k % 2][0:CC, :].rearrange("p (a c) -> p a c", a=4),
                                            heads(Bhi, k - 4), ALU.subtract).then_inc(s_abl, 1)
            @over_chunks(dve)
            def _(i):
                wait(dve, s_x1T, i)
                dve_norm(i, 0, s_xn1)
                dve.wait_ge(s_x1h, i + 1)
                nc.vector.tensor_tensor(x1l[:, bass.ds(T * i, T)], bank[4][:, :], x1h[:, bass.ds(T * i, T)],
                                        ALU.subtract).then_inc(s_x1l, 1)
            dve_cT(0, 0)
            for c in range(QT):
                dve_q(c, 0, c)
            dve.wait_ge(s_bo, 17)
            pipeline(nc.vector, dve_step)

            dve.wait_ge(s_res, G)
            base = LS
            dve_stats(chain, base)
            dve_rstd(chain, 2)
            dve.wait_ge(s_w2, 16 * (7 + 2 * HS))
            chain.link(nc.vector.tensor_scalar(omm[:, :], mix[:, :], -1.0, 1.0, ALU.mult, ALU.add))
            dve.wait_ge(s_texp, 1)
            nc.vector.tensor_scalar(nlw2[:, :], nlw[:, :], -1.0, None, ALU.mult).then_inc(s_tdve, 1)
            dve.wait_ge(s_texp, 2)
            chain.link(nc.vector.reciprocal(iap[:, :], apw[:, :]))
            dve.wait_ge(s_tab, 9)
            m = Chain(dve, s_m["ch"])
            per = 12
            @over_chunks(dve)
            def _(i):
                m.at(per * i)
                dve_norm(i, 0, s_m["xn"])
                dve.wait_ge(s_m["tmp"], i + 1)
                for k in range(3):
                    last = nc.vector.scalar_tensor_tensor(xm3[:, k, :].rearrange("p (s n) -> p s n", n=N),
                                                          xT33[:, :, 1:N + 1], mix[:, k:k + 1],
                                                          tmp3[:, k, :].rearrange("p (s n) -> p s n", n=N),
                                                          ALU.mult, ALU.add)
                last.then_inc(s_m["mix"], 1)
                v3 = lambda a: a.rearrange("p (s n) -> p s n", n=N)
                inv = iap[:, 1:N + 1].unsqueeze(1).broadcast_to([P, SEQ, N])
                dve.wait_ge(s_m["ek"], i + 1)
                dve.wait_ge(s_m["kvr"], 3 * i + 2)
                m.link(nc.vector.tensor_tensor(ekv[:, :], ek[:, :], bank[2][:, :], ALU.mult))
                m.mark(nc.vector.tensor_tensor(v3(fab[:, 0, :]), v3(ekv[:, :]), inv, ALU.mult))
                dve.wait_ge(s_m["sum"], i + 1)
                m.link(nc.vector.tensor_tensor(v3(fab[:, 1, :]), v3(bank[4][:, :]), inv, ALU.mult))
                wait(dve, s_m["st"], 2 * i)
                for k in range(2):
                    for s in range(SEQ):
                        last = nc.vector.tensor_tensor_scan(cs[:, k, s, 1:N + 1], onesn[:, :],
                                                            fab[:, k, s * N:(s + 1) * N], 0.0, ALU.mult, ALU.add)
                    last.then_inc(s_m["cs"], 1)
                for k in range(2):
                    dve.wait_ge(s_m["st"], 2 * i + k + 1)
                    m.link(nc.vector.tensor_scalar(scl[:, k, :], sraw[:, k, :], -FMAX, FMAX, ALU.max, ALU.min))
                    m.link(nc.vector.scalar_tensor_tensor(sst[:, k, :], sraw[:, k, :], FMAX, scl[:, k, :],
                                                          ALU.is_le, ALU.mult))
                m.mark(nc.vector.scalar_tensor_tensor(num[:, :], ekv[:, :], nlw[:, 1:2], sst[:, 0, :], ALU.mult, ALU.add))
                m.link(nc.vector.scalar_tensor_tensor(den[:, :], bank[4][:, :], nlw[:, 1:2], sst[:, 1, :],
                                                      ALU.mult, ALU.add))
                m.link(nc.vector.tensor_scalar(dmx[:, :], den[:, :], 1e-6, None, ALU.max))
                dve.wait_ge(s_m["er"], i + 1)
                m.link(nc.vector.scalar_tensor_tensor(rec[:, :], er[:, :], 1.0, dmx[:, :], ALU.add, ALU.mult))
                m.link(nc.vector.reciprocal(den[:, :], rec[:, :]))
                nc.vector.tensor_tensor(oT[:, :], num[:, :], den[:, :], ALU.mult).then_inc(s_m["o"], 1)
                assert m.count == per
                dve.wait_ge(s_m["y"], i + 1)
                xc = X[:, bass.ds(CT * i, CT), :].rearrange("p t c -> p (t c)")
                nc.vector.tensor_tensor(xc, xc, bank[5][:, :], ALU.add).then_inc(s_m["res"], 1)

            dve.wait_ge(s_m["res"], CH)
            dve_stats(chain, base + LS + 2)
            dve_rstd(chain, 3)
            dve.wait_ge(s_w3, 16 * 4)
            f = Chain(dve, s_f["ch"])
            per3 = 5
            @over_chunks(dve)
            def _(i):
                f.at(per3 * i)
                dve_norm(i, 0, s_f["xn"])
                dve.wait_ge(s_f["lg"], i + 1)
                f.link(nc.vector.tensor_tensor(lg[:, :, :], bank[1][:, 0:CT * E].rearrange("p (t e) -> p t e", e=E),
                                               brb[:, :].unsqueeze(1).broadcast_to([P, CT, E]), ALU.add))
                f.link(nc.vector.tensor_reduce(mx[:, :], lg[:, :, :], AX.X, ALU.max))
                f.link(nc.vector.tensor_tensor(eq[:, :, :], lg[:, :, :], mx[:, :].unsqueeze(2).broadcast_to([P, CT, E]),
                                               ALU.is_equal))
                f.link(nc.vector.tensor_tensor(wt[:, :, :], eq[:, :, :], desc[:, :].unsqueeze(1).broadcast_to([P, CT, E]),
                                               ALU.mult))
                f.link(nc.vector.tensor_reduce(mx[:, :], wt[:, :, :], AX.X, ALU.max))
                nc.vector.tensor_tensor(eq[:, :, :], wt[:, :, :], mx[:, :].unsqueeze(2).broadcast_to([P, CT, E]),
                                        ALU.is_equal).then_inc(s_f["eq"], 1)
                dve.wait_ge(s_f["eq"], i + 1)
                for e in range(E):
                    dve.wait_ge(s_f["y"], E * i + e + 1)
                    wait(dve, s_f["acc"], E * i + e)
                    for t in range(CT):
                        xc = X[:, bass.ds(CT * i + t, 1), :].rearrange("p o c -> p (o c)")
                        last = nc.vector.scalar_tensor_tensor(xc, bank[6 + e % 2][:, t * P:(t + 1) * P],
                                                              eq[:, t, e:e + 1], xc, ALU.mult, ALU.add)
                    last.then_inc(s_f["acc"], 1)


_INS = ['x', 'ctx_768', 'L0_xattn_Wq', 'L0_xattn_Wk', 'L0_xattn_Wv', 'L0_xattn_Wo', 'L0_xattn_bo',
        'L0_attn_mix_k', 'L0_attn_mix_v', 'L0_attn_mix_r', 'L0_attn_W_key', 'L0_attn_W_value',
        'L0_attn_W_receptance', 'L0_attn_W_output', 'L0_attn_time_decay', 'L0_attn_time_first',
        'L0_ffn_Wr', 'L0_ffn_br', 'L0_ffn_W1', 'L0_ffn_b1', 'L0_ffn_W2', 'L0_ffn_b2']
_OUTS = [((128, 32, 128), 'float32')]


def kernel(**inputs):
    import numpy as _np
    import concourse.bacc as _bacc
    from concourse import mybir as _mybir
    from concourse.bass_utils import run_bass_kernel_spmd as _run

    nc = _bacc.Bacc("TRN2", target_bir_lowering=False, num_devices=1)
    arrays, args = {}, []
    for name in _INS:
        a = _np.ascontiguousarray(inputs[name])
        arrays[f"in_{name}_dram"] = a
        args.append(nc.dram_tensor(f"in_{name}_dram", a.shape, _mybir.dt.from_np(a.dtype), kind="ExternalInput").ap())
    for i, (shape, dtype) in enumerate(_OUTS):
        dt = _mybir.dt.from_np(_np.dtype(dtype))
        args.append(nc.dram_tensor(f"out_{i}_dram", shape, dt, kind="ExternalOutput").ap())
    perceiver_layer_kernel(nc, *args)
    r = _run(nc, [arrays], core_ids=[0])
    return r.results[0]["out_0_dram"]
```

```python
from contextlib import ExitStack

import concourse.bass as bass
from concourse import mybir

ALU = mybir.AluOpType
ACT = mybir.ActivationFunctionType
AX = mybir.AxisListType
F32 = mybir.dt.float32
F16 = mybir.dt.float16
I32 = mybir.dt.int32
U32 = mybir.dt.uint32


P = 128
EPS = 1e-5
FMAX = 3.4028234663852886e38


def wait(eng, sem, value):
    if isinstance(value, int) and value <= 0:
        return
    eng.wait_ge(sem, value)


class Chain:

    def __init__(self, eng, sem):
        self.eng, self.sem, self.base, self.count = eng, sem, 0, 0

    def at(self, base):
        self.base, self.count = base, 0

    def link(self, ins):
        self.count += 1
        ins.then_inc(self.sem, 1)
        self.eng.wait_ge(self.sem, self.base + self.count)

    def mark(self, ins):
        self.count += 1
        ins.then_inc(self.sem, 1)


def perceiver_layer_kernel(nc, x, ctx, Wq, Wk, Wv, Wo, bo, mix_k, mix_v, mix_r, W_key, W_value,
                           W_rec, W_out, decay, first, Wr, br, W1, b1, W2, b2, out):
    B, N, C = x.shape
    _, M, CC = ctx.shape
    HD = Wq.shape[1]
    H = 16
    D = HD // H
    SCALE = float(D) ** -0.5
    TOK = B * N
    G = TOK // P
    GB = P // N
    QT = H * N // P
    Q = H * N
    MC = M // P
    LAST = M - 1
    assert M == MC * P + 1 and Q == 512
    NP2 = 2
    CH = 8
    CT = G // CH
    SEQ = CT * GB
    T = CT * P
    E = Wr.shape[0]
    FF = W1.shape[1]
    FC = FF // P
    HS = C // H
    R3 = 3
    LR = R3 * QT
    RW = C + 3
    NT = G + E
    UN = 4
    NV = UN + 3
    NK = NT // UN + 2
    FAR = 1 << 20

    top = ExitStack()

    def sb(name, shape, dt=F32):
        return top.enter_context(nc.sbuf_tensor(name, shape, dt))

    def sem(name):
        return top.enter_context(nc.semaphore(name))

    with top:
        bank = [top.enter_context(nc.psum_tensor(f"bank{i}", [P, 512], F32)) for i in range(8)]

        R = sb("R", [P, G, RW])
        X = R[:, :, 0:C]
        identf = sb("identf", [P, P])
        one = sb("one", [P, 1])
        ident = sb("ident", [P, P], F16)
        stats = sb("stats", [P, G, 6])
        mean = sb("mean", [P, G])
        std = sb("std", [P, G])
        rst = sb("rst", [P, G])
        tmpv = sb("tmpv", [P, G])
        varp = sb("varp", [P, G])
        xn = sb("xn", [P, 2, CT, C])
        w2r = sb("w2r", [P, 4, C])
        w2T = sb("w2T", [P, 4, C])
        wka = sb("wka", [P, C])
        wkb = sb("wkb", [P, C])
        mix = sb("mix", [P, 3])
        omm = sb("omm", [P, 1])
        dcy = sb("dcy", [P, 2])
        nlw = sb("nlw", [P, 2])
        nlw2 = sb("nlw2", [P, 2])
        tt = sb("tt", [P, N + 1])
        apw = sb("apw", [P, N + 1])
        iap = sb("iap", [P, N + 1])
        blk = sb("blk", [P, P])
        onesn = sb("onesn", [P, N])

        s_id = sem("s_id")
        s_const = sem("s_const")
        s_x = [sem(f"s_x{i}") for i in range(4)]
        s_var = sem("s_var")
        s_std = sem("s_std")
        s_ln = sem("s_ln")

        s_w = sem("s_w")
        s_wT = sem("s_wT")
        s_wTc = sem("s_wTc")
        s_ab = sem("s_ab")
        s_abh = sem("s_abh")
        s_abl = sem("s_abl")
        s_xn1 = sem("s_xn1")
        s_x1T = sem("s_x1T")
        s_x1h = sem("s_x1h")
        s_x1l = sem("s_x1l")
        s_bo = sem("s_bo")
        s_raw0 = sem("s_raw0")
        s_ctx = [sem(f"s_ctx{i}") for i in range(NP2)]
        s_chi = sem("s_chi")
        s_clo = sem("s_clo")
        s_c256 = sem("s_c256")
        s_ch = sem("s_ch")
        s_zd = sem("s_zd")
        s_z = [sem(f"s_z{i}") for i in range(NP2)]
        s_ctxT = sem("s_ctxT")
        s_cT = sem("s_cT")
        s_q = sem("s_q")
        s_qh = sem("s_qh")
        s_ql = sem("s_ql")
        s_S = sem("s_S")
        s_nmax = sem("s_nmax")
        s_exp = sem("s_exp")
        s_rs = sem("s_rs")
        s_pn = sem("s_pn")
        s_ehi = sem("s_ehi")
        s_elo = sem("s_elo")
        s_left = sem("s_left")
        s_L12 = sem("s_L12")
        s_T = sem("s_T")
        s_Th = sem("s_Th")
        s_Tl = sem("s_Tl")
        s_PV = sem("s_PV")
        s_Oh = sem("s_Oh")
        s_Ol = sem("s_Ol")
        s_y = sem("s_y")
        s_res = sem("s_res")
        s_w2 = sem("s_w2")
        s_w2T = sem("s_w2T")
        s_w2Tc = sem("s_w2Tc")
        s_tab = sem("s_tab")
        s_texp = sem("s_texp")
        s_tdve = sem("s_tdve")
        s_m = {n: sem("m_" + n) for n in ("w", "zero", "xn", "xT", "xc", "k", "v", "r", "ek", "er", "er1", "sum", "esum",
                                          "dx", "mdx", "xm", "ekv", "fab", "cs", "st", "rec", "o", "y", "res", "ch")}
        s_w3 = sem("s_w3")
        s_w3r = sem("s_w3r")
        s_w3T = sem("s_w3T")
        s_w3h = sem("s_w3h")
        s_w3l = sem("s_w3l")
        s_small = sem("s_small")
        s_smallT = sem("s_smallT")
        s_ftab = sem("s_ftab")
        s_fill = sem("s_fill")
        s_row = sem("s_row")
        s_hot = sem("s_hot")
        s_cnt = sem("s_cnt")
        s_pos = sem("s_pos")
        s_te = sem("s_te")
        s_sorted = sem("s_sorted")
        s_route = sem("s_route")
        s_f = {n: sem("f_" + n) for n in ("xn", "xT", "xc", "lg", "rt")}
        s_xs = [sem(f"s_xs{u}") for u in range(UN)]
        s_store = [sem(f"s_store{u}") for u in range(UN)]
        s_t = {n: sem("t_" + n) for n in ("xn", "xT", "xh", "xl", "h", "hr", "hh", "hl", "y", "yb", "out")}

        block = top.enter_context(nc.Block())

        arena = ExitStack()

        def asb(name, shape, dt=F32):
            return arena.enter_context(nc.sbuf_tensor(name, shape, dt))

        x1h = asb("x1h", [P, TOK], F16)
        x1l = asb("x1l", [P, TOK], F16)
        bob = asb("bob", [P, C])
        Ahi = asb("Ahi", [P, H, CC], F16)
        Alo = asb("Alo", [P, H, CC], F16)
        Bhi = asb("Bhi", [CC, H, C], F16)
        Blo = asb("Blo", [CC, H, C], F16)
        raw = asb("raw", [P, NP2, GB, MC + 1, CC])
        NC8 = NP2 * GB
        chi = asb("chi", [P, NC8, MC + 1, CC], F16)
        clo = asb("clo", [P, NC8, MC + 1, CC], F16)
        c256 = asb("c256", [P, CC])
        c256h = asb("c256h", [P, CC], F16)
        c256l = asb("c256l", [P, CC], F16)
        Z = asb("Z", [LR, NP2, GB, QT, CC], F16)
        MP = M + 1
        cT = asb("cT", [CC, 4, 2, MP], F16)
        qh = asb("qh", [CC, NP2, GB, Q], F16)
        ql = asb("ql", [CC, NP2, GB, Q], F16)
        nmax = asb("nmax", [P, NP2, QT])
        sums = asb("sums", [P, NP2, QT])
        rsum = asb("rsum", [P, NP2, QT])
        Pe = asb("Pe", [P, NP2, QT, M])
        Pn = asb("Pn", [P, NP2, QT, M])
        e12 = asb("e12", [P, NP2, R3, QT], F16)
        Th = asb("Th", [P, NP2, MC, Q], F16)
        Tl = asb("Tl", [P, NP2, MC, Q], F16)
        L12 = asb("L12", [LR, NP2, P], F16)
        Oh = asb("Oh", [CC, NP2, H, P], F16)
        Ol = asb("Ol", [CC, NP2, H, P], F16)
        warena = ExitStack()
        wq_r = warena.enter_context(nc.sbuf_tensor("wq_r", [P, HD], F32))
        wk_r = warena.enter_context(nc.sbuf_tensor("wk_r", [CC, HD], F32))
        wv_r = warena.enter_context(nc.sbuf_tensor("wv_r", [CC, HD], F32))
        wo_r = warena.enter_context(nc.sbuf_tensor("wo_r", [P, H // 2, C], F32))
        wqT = warena.enter_context(nc.sbuf_tensor("wqT", [P, H // 2, P], F32))
        wkT = warena.enter_context(nc.sbuf_tensor("wkT", [P, H // 2, CC], F32))
        wvT = warena.enter_context(nc.sbuf_tensor("wvT", [P, H // 2, CC], F32))
        warena.close()
        arena.close()

        late = ExitStack()

        def lsb(name, shape, dt=F32):
            return late.enter_context(nc.sbuf_tensor(name, shape, dt))

        xT33 = lsb("xT33", [P, 2, SEQ, N + 1])
        dx = lsb("dx", [P, T])
        mdx = lsb("mdx", [P, 2, T])
        xm = lsb("xm", [P, 2, 2, T])
        ek = lsb("ek", [P, 2, T])
        er = lsb("er", [P, 2, T])
        er1 = lsb("er1", [P, 2, T])
        esum = lsb("esum", [P, 2, T])
        ekv = lsb("ekv", [P, 2, T])
        fab = lsb("fab", [P, 2, T])
        cs = lsb("cs", [P, 2, SEQ, N + 1])
        sraw = lsb("sraw", [P, 2, T])
        scl = lsb("scl", [P, 2, T])
        sst = lsb("sst", [P, 2, T])
        num = lsb("num", [P, 2, T])
        den = lsb("den", [P, T])
        rec = lsb("rec", [P, 2, T])
        oT = lsb("oT", [P, T])
        w1r = lsb("w1r", [P, E, FC, C])
        w2fr = lsb("w2fr", [P, E, FF])
        W1h = lsb("W1h", [P, E, FF], F16)
        W1l = lsb("W1l", [P, E, FF], F16)
        W2h = lsb("W2h", [P, E, FF], F16)
        W2l = lsb("W2l", [P, E, FF], F16)
        wrr = lsb("wrr", [E, C])
        wrT = lsb("wrT", [P, E])
        brb = lsb("brb", [P, E])
        b1r = lsb("b1r", [E * FC, P])
        b1T = lsb("b1T", [P, E * FC])
        b2b = lsb("b2b", [P, E, C + 1])
        desc = lsb("desc", [P, E])
        tri = lsb("tri", [P, P], F16)
        onesh = lsb("onesh", [P, P], F16)
        onesr = lsb("onesr", [P, G])
        kk = lsb("kk", [P, E, G])
        ti = lsb("ti", [P, NT, E])
        fill = lsb("fill", [P, RW])
        x3T = lsb("x3T", [P, 2, T])
        lg = lsb("lg", [P, G, E])
        eq = lsb("eq", [P, G, E])
        wt = lsb("wt", [P, G, E])
        hot = lsb("hot", [P, G, E], F16)
        mx = lsb("mx", [P, G])
        cnt = lsb("cnt", [P, G, E])
        run = lsb("run", [P, G, E])
        before = lsb("before", [P, G, E])
        slot = lsb("slot", [P, G, E])
        gt = lsb("gt", [P, E, G])
        tiles = lsb("tiles", [P, E])
        ends = lsb("ends", [P, E])
        offs = lsb("offs", [P, E])
        ge = lsb("ge", [P, NT, E])
        te = lsb("te", [P, NT])
        tep = lsb("tep", [P, UN * NK + NV])
        pkf = lsb("pkf", [P, NK])
        pk = lsb("pk", [P, NK], I32)
        posf = lsb("posf", [P, G])
        pos = lsb("pos", [P, G], U32)
        xs = lsb("xs", [P, UN, RW])
        xsn = lsb("xsn", [P, 2, C])
        xsh = lsb("xsh", [P, 2, P], F16)
        xsl = lsb("xsl", [P, 2, P], F16)
        hr = lsb("hr", [P, 2, FC, P])
        hh = lsb("hh", [P, UN, FC, P], F16)
        hl = lsb("hl", [P, UN, FC, P], F16)
        yb = lsb("yb", [P, UN, C + 1])
        yout = lsb("yout", [P, UN, C])
        idx = lsb("idx", [P, UN], U32)
        late.close()

        bankh = [b[:, :].bitcast(F16) for b in bank]

        zdram = nc.dram_tensor("last_rows", [R3, B, CC], F16, kind="Internal").ap()
        SB = (0, 1, 2, 0)
        xt_dram = x.rearrange("(g b) n c -> (b n) g c", b=GB)
        out_rows = out.rearrange("b n c -> (b n) c")
        sorted_rows = nc.dram_tensor("sorted_rows", [NT * P, RW], F32, kind="Internal").ap()
        ctx_main = ctx[:, 0:MC * P, :].rearrange("b (p s) c -> p b s c", s=MC)
        col = lambda a: a.rearrange("a b c -> c (a b)")

        def heads(buf, k):
            return buf[:, :, :].rearrange("p (q two) c -> p two q c", two=2)[:, k % 2, 4 * (k // 2):4 * (k // 2) + 4, :]


        def where(it, j):
            return 8 * it + j, 2 * it + j // GB, j % GB, (j // GB) % NP2

        def pe_ctxT(n, s8, s4):
            wait(nc.tensor, s_clo, n + 1)
            wait(nc.tensor, s_cT, n)
            wait(nc.tensor, s_L12, n - 2)
            for half, src in enumerate((chi, clo)):
                for c in range(MC):
                    nc.tensor.transpose(bankh[7][0:CC, half * MP + c * P:half * MP + (c + 1) * P],
                                        src[:, s8, c, :], ident[:, :])
                last = nc.tensor.transpose(bankh[7][0:CC, half * MP + MC * P:half * MP + MC * P + 2],
                                           src[0:2, s8, MC, :], ident[0:2, 0:2])
            last.then_inc(s_ctxT, 1)

        def pe_scores(n, par, b, s4, tiles):
            wait(nc.tensor, s_cT, n + 1)
            for t in tiles:
                wait(nc.tensor, s_exp, QT * n + 1 if t == 3 else QT * (n - 1) + (t or 3) + 1)
                for k, (w, c) in enumerate(((qh, 0), (qh, 1), (ql, 0))):
                    last = nc.tensor.matmul(bank[SB[t]][:, 0:M], w[:, par, b, t * P:(t + 1) * P],
                                            cT[:, s4, c, 0:M], start=(k == 0), stop=(k == 2))
                last.then_inc(s_S, 1)

        QB = (0, 1, 6, 0)

        def pe_q(k, c, tok, b=3, free=None):
            wait(nc.tensor, s_ql, k if free is None else free)
            for hh in range(QT):
                h = QT * c + hh
                for k, (w, a) in enumerate(((Ahi, x1h), (Ahi, x1l), (Alo, x1h))):
                    last = nc.tensor.matmul(bank[b][0:CC, hh * P:(hh + 1) * P], w[:, h, :], a[:, tok],
                                            start=(k == 0), stop=(k == 2))
            last.then_inc(s_q, 1)

        def pe_pv(n, par, s8, gp, b, pairs):
            wait(nc.tensor, s_Ol, n)
            k = 0
            for w, p, s in ((chi, Th, s_Th), (clo, Th, None), (chi, Tl, s_Tl)):
                for c in range(MC):
                    if s is not None:
                        wait(nc.tensor, s, MC * n + c + 1)
                    nc.tensor.matmul(bank[6][0:CC, :], w[:, s8, c, :], p[:, par, c, :], start=(k == 0), stop=False)
                    k += 1
            wait(nc.tensor, s_L12, n + 1)
            if b == 0:
                wait(nc.tensor, s_z[gp], 16 * QT * pairs)
            for t in range(QT):
                last = nc.tensor.matmul(bank[6][0:CC, t * P:(t + 1) * P], Z[:, gp, b, t, :], L12[:, par, :],
                                        start=False, stop=(t == QT - 1))
            last.then_inc(s_PV, 1)

        def pe_y(g, gp):
            wait(nc.tensor, s_Ol, GB * (g + 1))
            for h in range(H):
                for k, (o, w) in enumerate(((Oh, Bhi), (Oh, Blo), (Ol, Bhi))):
                    last = nc.tensor.matmul(bank[7][:, 512 - C:512], o[:, gp, h, :], w[:, h, :],
                                            start=(h == 0 and k == 0), stop=(h == H - 1 and k == 2))
            last.then_inc(s_y, 1)

        def pe_probsT(n, par):
            for c in range(MC):
                wait(nc.tensor, s_Tl, MC * (n - 1) + c + 1)
                for t in range(QT):
                    last = nc.tensor.transpose(bank[4 + c][:, t * P:(t + 1) * P], Pn[:, par, t, c * P:(c + 1) * P],
                                               identf[:, :])
                last.then_inc(s_T, 1)

        def exists(n, last=B):
            return not isinstance(n, int) or 0 <= n < last

        def pe_step(it, j):
            n, g, jj, gp = where(it, j)
            if jj == 2 and exists(g - 1, G):
                wait(nc.tensor, s_res, g)
            if exists(n + 2):
                pe_ctxT(n + 2, (j + 2) % NC8, (j + 2) % 4)
            if exists(n + 1):
                if (j + 1) % GB == 0:
                    wait(nc.tensor, s_ql, n + 5)
                pe_scores(n + 1, ((j + 1) // GB) % NP2, (j + 1) % GB, (j + 1) % 4, (0, 1, 2))
            if exists(n + 5):
                pe_q(n + 5, (j + 1) % GB, bass.ds(P * (g + 1 + (jj + 1) // GB), P))
            if exists(n + 1):
                pe_scores(n + 1, ((j + 1) // GB) % NP2, (j + 1) % GB, (j + 1) % 4, (3,))
            if exists(n - 1):
                pe_pv(n - 1, (j - 1) % NP2, (j - 1) % NC8, ((j - 1) // GB) % NP2, (j - 1) % GB,
                      it + 1 + (j - 1) // NC8)
            if exists(n + 2):
                wait(nc.tensor, s_cT, n + 3)
            else:
                wait(nc.tensor, s_L12, min(n, B))
            if jj == 1 and exists(g - 1, G):
                pe_y(g - 1, 1 - gp)
            if exists(n):
                wait(nc.tensor, s_elo, n + 1)
                nc.tensor.transpose(bankh[7][0:LR, 0:P], e12[:, n_par(j), :, :].rearrange("p r t -> p (r t)"),
                                    ident[:, :]).then_inc(s_left, 1)
                wait(nc.tensor, s_pn, n + 1)
                pe_probsT(n, n_par(j))

        def n_par(j):
            return j % NP2

        def act_step(it, j):
            n, g, jj, gp = where(it, j)
            if exists(n - 1):
                wait(nc.scalar, s_PV, n - 2)
                for c in range(MC):
                    wait(nc.scalar, s_T, MC * (n - 1) + c + 1)
                    nc.scalar.activation(Th[:, n_par(j - 1), c, :], bank[4 + c][:, :], ACT.Copy).then_inc(s_Th, 1)
            for t in range(QT):
                if exists(n + 1):
                    if t == 0:
                        wait(nc.scalar, s_elo, n)
                    wait(nc.scalar, s_nmax, QT * (n + 1) + t + 1)
                    nc.scalar.activation(Pe[:, n_par(j + 1), t, :], bank[SB[t]][:, 0:M], ACT.Exp,
                                         bias=nmax[:, n_par(j + 1), t:t + 1],
                                         accum_out=sums[:, n_par(j + 1), t:t + 1]).then_inc(s_exp, 1)
                if t == 2 and exists(n + 5):
                    act_q(n + 5, (gp + 1 + (jj + 1) // GB) % NP2, (j + 1) % GB)
            if exists(n - 1):
                if (j - 1) % GB == 0:
                    wait(nc.scalar, s_y, g - 1)
                wait(nc.scalar, s_PV, n)
                nc.scalar.activation(Oh[:, ((j - 1) // GB) % NP2, :, ((j - 1) % GB) * N:((j - 1) % GB + 1) * N],
                                     bank[6][0:CC, :].rearrange("p (h t) -> p h t", h=H), ACT.Copy).then_inc(s_Oh, 1)

        def q_view(buf, par, c):
            return buf[:, par, :, c * P:(c + 1) * P].rearrange("p b (h t) -> p h b t", h=QT)

        def act_q(k, par, c, b=3):
            wait(nc.scalar, s_q, k + 1)
            wait(nc.scalar, s_S, QT * (k - c) - QT * GB)
            nc.scalar.activation(q_view(qh, par, c), bank[b][0:CC, :].rearrange("p (h b t) -> p h b t", h=QT, b=GB),
                                 ACT.Copy).then_inc(s_qh, 1)

        def dve_q(k, par, c, b=3):
            wait(nc.vector, s_qh, k + 1)
            nc.vector.tensor_tensor(q_view(ql, par, c), bank[b][0:CC, :].rearrange("p (h b t) -> p h b t", h=QT, b=GB),
                                    q_view(qh, par, c), ALU.subtract).then_inc(s_ql, 1)

        def dve_step(it, j):
            n, g, jj, gp = where(it, j)
            moments = jj == 2 and exists(g - 1, G)
            if moments:
                wait(nc.vector, s_res, g)
            if exists(n + 2):
                dve_cT(n + 2, (j + 2) % 4)
            if moments:
                dve_stats(g - 1)
            for kind, t in (("max", 0), ("max", 1), ("low", 0), ("max", 2), ("low", 1), ("max", 3)):
                if kind == "low" and exists(n - 1):
                    wait(nc.vector, s_Th, MC * (n - 1) + t + 1)
                    nc.vector.tensor_tensor(Tl[:, n_par(j - 1), t, :], bank[4 + t][:, :], Th[:, n_par(j - 1), t, :],
                                            ALU.subtract).then_inc(s_Tl, 1)
                if kind == "max" and exists(n + 1):
                    wait(nc.vector, s_S, QT * (n + 1) + t + 1)
                    nc.vector.tensor_reduce(nmax[:, n_par(j + 1), t:t + 1], bank[SB[t]][:, 0:M], AX.X, ALU.max,
                                            negate=True).then_inc(s_nmax, 1)
            if exists(n + 5):
                dve_q(n + 5, (gp + 1 + (jj + 1) // GB) % NP2, (j + 1) % GB)
            if exists(n + 1):
                wait(nc.vector, s_exp, QT * (n + 2))
                wait(nc.vector, s_pn, n)
                nc.vector.reciprocal(rsum[:, n_par(j + 1), :], sums[:, n_par(j + 1), :]).then_inc(s_rs, 1)
            if exists(n):
                wait(nc.vector, s_left, n + 1)
                wait(nc.vector, s_PV, n - 1)
                nc.vector.tensor_copy(L12[:, n_par(j), :], bankh[7][0:LR, 0:P]).then_inc(s_L12, 1)
            if jj == 1 and exists(g - 1, G):
                wait(nc.vector, s_y, g)
                tile = X[:, bass.ds(g - 1, 1), :].rearrange("p o c -> p (o c)")
                nc.vector.tensor_tensor(tile, tile, bank[7][:, 512 - C:512], ALU.add).then_inc(s_res, 1)
            if exists(n - 1):
                wait(nc.vector, s_Oh, n)
                sl = (slice(None), ((j - 1) // GB) % NP2, slice(None), slice(((j - 1) % GB) * N, ((j - 1) % GB + 1) * N))
                nc.vector.tensor_tensor(Ol[sl], bank[6][0:CC, :].rearrange("p (h t) -> p h t", h=H), Oh[sl],
                                        ALU.subtract).then_inc(s_Ol, 1)

        def dve_cT(n, s4):
            wait(nc.vector, s_ctxT, n + 1)
            nc.vector.tensor_copy(cT[:, s4, :, :].rearrange("p s m -> p (s m)"), bankh[7][0:CC, 0:2 * MP])\
                .then_inc(s_cT, 1)

        def pool_prep(n, s8, par, b):
            wait(nc.gpsimd, s_PV, n - 7)
            nc.gpsimd.tensor_tensor(chi[:, s8, :, :], raw[:, par, b, :, :],
                                    one[:, 0:1].unsqueeze(2).broadcast_to([P, MC + 1, CC]), ALU.mult)\
                .then_inc(s_chi, 1)
            wait(nc.gpsimd, s_chi, n + 1)
            nc.gpsimd.tensor_tensor(clo[:, s8, :, :], raw[:, par, b, :, :], chi[:, s8, :, :], ALU.subtract)\
                .then_inc(s_clo, 1)

        def pool_step(it, j):
            n, g, jj, gp = where(it, j)
            if exists(n + 1):
                wait(nc.gpsimd, s_rs, n + 2)
                wait(nc.gpsimd, s_T, MC * n)
                par = n_par(j + 1)
                nc.gpsimd.tensor_tensor(Pn[:, par, :, :], Pe[:, par, :, :],
                                        rsum[:, par, :].unsqueeze(2).broadcast_to([P, QT, M]), ALU.mult)\
                    .then_inc(s_pn, 1)
                wait(nc.gpsimd, s_pn, n + 2)
                wait(nc.gpsimd, s_left, n)
                lastcol = Pn[:, par, :, LAST:M].rearrange("p t o -> p (t o)")
                nc.gpsimd.tensor_tensor(e12[:, par, 0:R3:2, :], lastcol.unsqueeze(1).broadcast_to([P, 2, QT]),
                                        one[:, 0:1].unsqueeze(2).broadcast_to([P, 2, QT]), ALU.mult).then_inc(s_ehi, 1)
                wait(nc.gpsimd, s_ehi, n + 2)
                nc.gpsimd.tensor_tensor(e12[:, par, 1, :], lastcol, e12[:, par, 0, :], ALU.subtract).then_inc(s_elo, 1)
            if exists(n + 4):
                if (j + 4) % GB == 0:
                    wait(nc.gpsimd, s_ctx[((j + 4) // GB) % NP2], 32 * (it + 1 + ((j + 4) // GB - ((j + 4) // GB) % NP2) // NP2))
                pool_prep(n + 4, (j + 4) % NC8, ((j + 4) // GB) % NP2, (j + 4) % GB)

        def pipeline(eng, step):
            for j in range(-1, 7):
                step(0, j)
            with eng.Fori(1, B // 8 - 1) as it:
                for j in range(-1, 7):
                    step(it, j)
            for j in range(-1, 10):
                step(B // 8 - 1, j)

        def time(a):
            return a.rearrange("p (s n) -> p s n", n=N)

        def over_seqs(a):
            return a.unsqueeze(1).broadcast_to([P, SEQ, N])

        def over_pairs(step):
            def run(eng):
                for u in range(-2, 2):
                    step(0, u)
                with eng.Fori(1, CH // 2 - 1) as it:
                    for u in range(2):
                        step(it, u)
                for u in range(4):
                    step(CH // 2 - 1, u)
            return run

        def over_tiles(eng, step, routed=True):
            def block(it):
                pack = eng.value_load(pk[0:1, bass.ds(it, 1)], min_val=0, max_val=E ** NV - 1) if routed else None
                for u in range(1 - UN, 1):
                    step(it, u, lambda v: (pack // E ** (v + 5)) % E)
            for it in range(3):
                block(it)
            with eng.Fori(3, NT // UN) as it:
                block(it)
            for it in range(NT // UN, NK):
                block(it)

        LS = G + 6 + 5

        def dve_stats(k):
            nc.vector.bn_stats(stats[:, bass.ds(k, 1), :].rearrange("p o s -> p (o s)"),
                               X[:, bass.ds(k, 1), :].rearrange("p o c -> p (o c)")).then_inc(s_ln, 1)

        def dve_var(chain, base):
            chain.at(base + G)
            nc.vector.wait_ge(chain.sem, base + G)
            chain.mark(nc.vector.tensor_tensor(tmpv[:, :], stats[:, :, 1], stats[:, :, 4], ALU.add))
            chain.mark(nc.vector.tensor_tensor(std[:, :], stats[:, :, 1], stats[:, :, 4], ALU.subtract))
            chain.link(nc.vector.tensor_tensor(rst[:, :], stats[:, :, 2], stats[:, :, 5], ALU.add))
            chain.mark(nc.vector.tensor_scalar(mean[:, :], tmpv[:, :], 0.5, None, ALU.mult))
            chain.link(nc.vector.scalar_tensor_tensor(varp[:, :], std[:, :], 0.25, std[:, :], ALU.mult, ALU.mult))
            chain.link(nc.vector.tensor_scalar(tmpv[:, :], rst[:, :], 1.0 / C, EPS, ALU.mult, ALU.add))

        def dve_rstd(chain, phase):
            nc.vector.tensor_tensor(varp[:, :], varp[:, :], tmpv[:, :], ALU.add).then_inc(s_var, 1)
            nc.vector.wait_ge(s_var, phase)
            nc.vector.wait_ge(s_std, phase)
            chain.link(nc.vector.reciprocal(rst[:, :], std[:, :]))
            chain.link(nc.vector.tensor_tensor(tmpv[:, :], rst[:, :], rst[:, :], ALU.mult))
            chain.link(nc.vector.tensor_tensor(tmpv[:, :], tmpv[:, :], varp[:, :], ALU.mult))
            chain.link(nc.vector.tensor_scalar(tmpv[:, :], tmpv[:, :], -0.5, 1.5, ALU.mult, ALU.add))
            chain.link(nc.vector.tensor_tensor(rst[:, :], rst[:, :], tmpv[:, :], ALU.mult))

        def act_std(phase):
            nc.scalar.wait_ge(s_var, phase)
            nc.scalar.activation(std[:, :], varp[:, :], ACT.Sqrt).then_inc(s_std, 1)

        def dve_norm(i, par, s):
            for t in range(CT):
                k = CT * i + t
                last = nc.vector.tensor_scalar(xn[:, par, t, :], X[:, bass.ds(k, 1), :].rearrange("p o c -> p (o c)"),
                                               mean[:, bass.ds(k, 1)],
                                               rst[:, bass.ds(k, 1)], ALU.subtract, ALU.mult)
            last.then_inc(s, 1)

        def pe_norm_T(par, b, s):
            for t in range(CT):
                last = nc.tensor.transpose(bank[b][:, t * P:(t + 1) * P], xn[:, par, t, :], identf[:, :])
            last.then_inc(s, 1)

        @block.sync
        def _(sp):
            GX = G // 4
            for i in range(4):
                sp.dma_start(X[:, GX * i:GX * (i + 1), :], xt_dram[:, GX * i:GX * (i + 1), :]).then_inc(s_x[i], 16)
            sp.dma_start(wq_r[:, :], Wq).then_inc(s_w, 16)
            sp.dma_start(wk_r[:, :], Wk).then_inc(s_w, 16)
            sp.dma_start(wv_r[:, :], Wv).then_inc(s_w, 16)
            sp.dma_start(wo_r[:, :, :], Wo.rearrange("(a p) c -> p a c", p=P)).then_inc(s_w, 16)
            sp.dma_start(bob[:, :], bo.rearrange("(o c) -> o c", o=1).broadcast_to([P, C])).then_inc(s_bo, 16)
            sp.dma_start(c256[:, :], ctx[:, LAST, :]).then_inc(s_c256, 16)
            sp.wait_ge(s_raw0, 2)

            def load_ctx(g, par):
                b0 = GB * g
                wait(sp, s_clo, GB * (g - 1))
                sp.dma_start(raw[:, par, :, 0:MC, :], ctx_main[:, bass.ds(b0, GB), :, :]).then_inc(s_ctx[par], 16)
                sp.dma_start(raw[0:1, par, :, MC, :], ctx[bass.ds(b0, GB), LAST:M, :].rearrange("b o c -> o b c"))\
                    .then_inc(s_ctx[par], 16)

            def load_z(g, par):
                wait(sp, s_PV, GB * (g - 1))
                for t in range(QT):
                    sp.dma_start(Z[t:LR:QT, par, :, t, :], zdram[:, bass.ds(GB * g, GB), :]).then_inc(s_z[par], 16)

            load_ctx(0, 0)
            load_ctx(1, 1)
            sp.wait_ge(s_ch, 2)
            for r, part in enumerate((c256h, c256h, c256l)):
                sp.dma_start(zdram[r], part[:, :]).then_inc(s_zd, 16)
            sp.wait_ge(s_zd, 16 * R3)
            load_z(0, 0)
            load_z(1, 1)
            for i, w in enumerate((W_key, W_value, W_rec, W_out)):
                sp.dma_start(w2r[:, i, :], w).then_inc(s_w2, 16)
            for i, m in enumerate((mix_k, mix_v, mix_r)):
                sp.dma_start(mix[:, i:i + 1], col(m)).then_inc(s_w2, 16)
            for i, v in enumerate((decay, first)):
                for a in range(HS):
                    sp.dma_start(dcy[a:P:HS, i:i + 1], v.rearrange("(h o) -> h o", o=1)).then_inc(s_w2, 16)
            with sp.Fori(1, G // 2) as i:
                for par in range(NP2):
                    load_ctx(2 * i + par, par)
                    load_z(2 * i + par, par)
            sp.wait_ge(s_res, G)
            sp.dma_start(wrr[:, :], Wr).then_inc(s_small, 16)
            sp.dma_start(b1r[:, :], b1.rearrange("e (f p) -> (e f) p", p=P)).then_inc(s_small, 16)
            sp.dma_start(brb[:, :], br.rearrange("(o e) -> o e", o=1).broadcast_to([P, E])).then_inc(s_w3, 16)
            sp.dma_start(b2b[:, :, 0:C], b2.rearrange("(o e) d -> o e d", o=1).broadcast_to([P, E, C])).then_inc(s_w3, 16)
            sp.wait_ge(s_ftab, 8)
            sp.dma_start(sorted_rows.rearrange("(t p) c -> p t c", p=P),
                         fill[:, :].unsqueeze(1).broadcast_to([P, NT, RW])).then_inc(s_fill, 16)
            for e in range(E):
                sp.dma_start(w1r[:, e, :, :], W1[e].rearrange("(f p) d -> p f d", p=P)).then_inc(s_w3r, 16)
                sp.dma_start(w2fr[:, e, :], W2[e]).then_inc(s_w3r, 16)
            sp.wait_ge(s_sorted, 16 * G)

            def load_tile(s, u):
                wait(sp, s_t["xn"], s - UN + 1)
                wait(sp, s_t["yb"], s - UN + 1)
                sp.dma_start(xs[:, u, :], sorted_rows[bass.ds(P * s, P), :]).then_inc(s_xs[u], 16)

            for u in range(UN):
                load_tile(u, u)
            with sp.Fori(1, NT // UN) as i:
                for u in range(UN):
                    load_tile(UN * i + u, u)
            for u in range(UN):
                sp.wait_ge(s_store[u], 16 * (NT // UN))

        @block.gpsimd
        def _(pool):
            nc.gpsimd.memset(identf[:, :], 0.0).then_inc(s_id, 1)
            nc.gpsimd.memset(one[:, :], 1.0).then_inc(s_id, 1)
            nc.gpsimd.memset(raw[:, :, :, MC, :], 0.0).then_inc(s_raw0, 1)
            nc.gpsimd.memset(Z[:, :, :, :, :], 0.0).then_inc(s_raw0, 1)
            pool.wait_ge(s_id, 2)
            nc.gpsimd.affine_select(out=identf[:, :], in_=identf[:, :], compare_op=ALU.not_equal, fill=1.0,
                                    base=0, pattern=[[-1, P]], channel_multiplier=1).then_inc(s_const, 1)
            pool.wait_ge(s_const, 1)
            nc.gpsimd.tensor_copy(ident[:, :], identf[:, :]).then_inc(s_const, 1)
            pool.wait_ge(s_const, 2)
            pool.wait_ge(s_c256, 16)
            nc.gpsimd.tensor_copy(c256h[:, :], c256[:, :]).then_inc(s_ch, 1)
            pool.wait_ge(s_ch, 1)
            nc.gpsimd.tensor_tensor(c256l[:, :], c256[:, :], c256h[:, :], ALU.subtract).then_inc(s_ch, 1)
            pool.wait_ge(s_ctx[0], 32)
            for b in range(GB - 1):
                pool_prep(b, b, 0, b)
            pool.wait_ge(s_bo, 16)
            for i in range(CH):
                pool.wait_ge(s_xn1, i + 1)
                xc = X[:, CT * i:CT * (i + 1), :]
                nc.gpsimd.tensor_tensor(xc, xc, bob[:, :].unsqueeze(1).broadcast_to([P, CT, C]), ALU.add)\
                    .then_inc(s_bo, 1)
            nc.gpsimd.iota(tt[:, :], pattern=[[1, N + 1]], base=0, channel_multiplier=0,
                           allow_small_or_imprecise_dtypes=True).then_inc(s_tab, 1)
            nc.gpsimd.memset(onesn[:, :], 1.0).then_inc(s_tab, 1)
            nc.gpsimd.memset(blk[:, :], 1.0).then_inc(s_tab, 1)
            pool.wait_ge(s_tab, 3)
            bv = blk[:, :].rearrange("p (h a) -> p h a", a=HS)
            nc.gpsimd.affine_select(out=bv, in_=bv, compare_op=ALU.is_ge, fill=0.0, base=0,
                                    pattern=[[-HS, H], [0, HS]], channel_multiplier=1).then_inc(s_tab, 1)
            pool.wait_ge(s_tab, 4)
            nc.gpsimd.affine_select(out=bv, in_=bv, compare_op=ALU.is_ge, fill=0.0, base=HS - 1,
                                    pattern=[[HS, H], [0, HS]], channel_multiplier=-1).then_inc(s_tab, 1)
            pipeline(nc.gpsimd, pool_step)

            pool.wait_ge(s_res, G)
            nc.gpsimd.memset(xT33[:, :, :, 0:1], 0.0).then_inc(s_m["zero"], 1)
            nc.gpsimd.memset(cs[:, :, :, 0:1], 0.0).then_inc(s_m["zero"], 1)
            nc.gpsimd.iota(desc[:, :], pattern=[[-1, E]], base=E, channel_multiplier=0,
                           allow_small_or_imprecise_dtypes=True).then_inc(s_m["zero"], 1)
            nc.gpsimd.memset(tri[:, :], 1.0).then_inc(s_ftab, 1)
            nc.gpsimd.memset(onesh[:, :], 1.0).then_inc(s_ftab, 1)
            nc.gpsimd.memset(onesr[:, :], 1.0).then_inc(s_ftab, 1)
            nc.gpsimd.memset(b2b[:, :, C:C + 1], 0.0).then_inc(s_ftab, 1)
            nc.gpsimd.memset(fill[:, :], 0.0).then_inc(s_ftab, 1)
            nc.gpsimd.iota(kk[:, :, :], pattern=[[0, E], [P, G]], base=0, channel_multiplier=0,
                           allow_small_or_imprecise_dtypes=True).then_inc(s_ftab, 1)
            nc.gpsimd.iota(ti[:, :, :], pattern=[[1, NT], [0, E]], base=0, channel_multiplier=0,
                           allow_small_or_imprecise_dtypes=True).then_inc(s_ftab, 1)
            pool.wait_ge(s_ftab, 7)
            nc.gpsimd.iota(fill[:, C:C + 1], pattern=[[1, 1]], base=FAR, channel_multiplier=1,
                           allow_small_or_imprecise_dtypes=True).then_inc(s_ftab, 1)
            nc.gpsimd.iota(R[:, :, C], pattern=[[P, G]], base=0, channel_multiplier=1,
                           allow_small_or_imprecise_dtypes=True).then_inc(s_ftab, 1)
            pool.wait_ge(s_ftab, 9)
            nc.gpsimd.affine_select(out=tri[:, :], in_=tri[:, :], compare_op=ALU.is_gt, fill=0.0, base=0,
                                    pattern=[[1, P]], channel_multiplier=-1).then_inc(s_ftab, 1)
            def pool_mix(it, u):
                s, p = 2 * it + u, u % 2
                if exists(s, CH):
                    for k in range(2):
                        wait(pool, s_m["ch"], 7 * (s - 1) + k + 3)
                        wait(pool, s_m["cs"], 2 * s + k + 1)
                        nc.gpsimd.tensor_tensor(time(sraw[:, k, :]), cs[:, k, :, 0:N], over_seqs(apw[:, 0:N]), ALU.mult)\
                            .then_inc(s_m["st"], 1)
                if exists(s + 2, CH):
                    wait(pool, s_m["mdx"], s + 2)
                    wait(pool, s_m["xc"], s + 3)
                    nc.gpsimd.tensor_tensor(time(dx[:, :]), xT33[:, p, :, 1:N + 1], xT33[:, p, :, 0:N], ALU.subtract)\
                        .then_inc(s_m["dx"], 1)
                if exists(s + 1, CH):
                    q = 1 - p
                    wait(pool, s_m["cs"], 2 * s + 2)
                    wait(pool, s_m["ekv"], s + 2)
                    nc.gpsimd.tensor_tensor(time(fab[:, 0, :]), time(ekv[:, q, :]), over_seqs(iap[:, 1:N + 1]), ALU.mult)\
                        .then_inc(s_m["fab"], 1)
                    wait(pool, s_m["esum"], s + 2)
                    nc.gpsimd.tensor_tensor(time(fab[:, 1, :]), time(esum[:, q, :]), over_seqs(iap[:, 1:N + 1]), ALU.mult)\
                        .then_inc(s_m["fab"], 1)
                if exists(s + 2, CH):
                    wait(pool, s_m["v"], s + 1)
                    wait(pool, s_m["r"], s + 1)
                    wait(pool, s_m["mdx"], s + 3)
                    for k in range(2):
                        nc.gpsimd.tensor_tensor(time(xm[:, p, k, :]), time(mdx[:, k, :]), xT33[:, p, :, 0:N], ALU.add)\
                            .then_inc(s_m["xm"], 1)
                if exists(s, CH):
                    wait(pool, s_m["y"], s)
                    wait(pool, s_m["rec"], s + 1)
                    nc.gpsimd.tensor_tensor(oT[:, :], num[:, p, :], rec[:, p, :], ALU.mult).then_inc(s_m["o"], 1)

            over_pairs(pool_mix)(pool)

            pool.wait_ge(s_fill, 16)
            pool.wait_ge(s_row, 2)
            pool.wait_ge(s_pos, 1)
            pool.wait_ge(s_te, 1)
            for g in range(G):
                nc.gpsimd.indirect_dma_start(sorted_rows, bass.IndirectOffsetOnAxis(ap=pos[:, g:g + 1], axis=0),
                                             R[:, g, :], None, bounds_check=NT * P - 1).then_inc(s_sorted, 16)

            def pool_tile(it, u, expert):
                s = UN * it + u
                if exists(s - 3, NT):
                    wait(pool, s_t["out"], s - 2)
                if exists(s + 1, NT):
                    w = (u + 1) % UN
                    e = expert(u + 1)
                    wait(pool, s_xs[w], 16 * (it + 1 + (u + 1) // UN))
                    pool.wait_ge(s_w3, 32)
                    nc.gpsimd.tensor_tensor(yb[:, w, :], xs[:, w, 0:C + 1],
                                            b2b[:, bass.ds(e, 1), :].rearrange("p o c -> p (o c)"), ALU.add)\
                        .then_inc(s_t["yb"], 1)
                if exists(s - 3, NT):
                    v = (u - 3) % UN
                    nc.gpsimd.indirect_dma_start(out_rows, bass.IndirectOffsetOnAxis(ap=idx[:, v:v + 1], axis=0),
                                                 yout[:, v, :], None, bounds_check=TOK - 1, oob_is_err=False)\
                        .then_inc(s_store[v], 16)

            over_tiles(pool, pool_tile)

        @block.scalar
        def _(act):
            act_std(1)
            for k in range(6):
                act.wait_ge(s_wT, k + 1)
                dst, w = ((wqT, P), (wkT, CC), (wvT, CC))[k // 2]
                nc.scalar.activation(dst[:, 4 * (k % 2):4 * (k % 2) + 4, :],
                                     bank[k % 2][:, 0:4 * w].rearrange("p (a c) -> p a c", a=4), ACT.Copy)\
                    .then_inc(s_wTc, 1)
            for k in range(CH):
                act.wait_ge(s_ab, k + 1)
                if k < 4:
                    nc.scalar.activation(heads(Ahi, k),
                                         bank[2 + k % 2][:, 0:4 * CC].rearrange("p (a c) -> p a c", a=4), ACT.Copy,
                                         scale=SCALE).then_inc(s_abh, 1)
                else:
                    nc.scalar.activation(heads(Bhi, k - 4),
                                         bank[2 + k % 2][0:CC, :].rearrange("p (a c) -> p a c", a=4), ACT.Copy)\
                        .then_inc(s_abh, 1)
                act.wait_ge(s_x1T, k + 1)
                nc.scalar.activation(x1h[:, T * k:T * (k + 1)], bank[4 + k % 2][:, :], ACT.Copy).then_inc(s_x1h, 1)
                if k >= CH - QT:
                    c = k - (CH - QT)
                    act_q(c, 0, c, QB[c])
            pipeline(nc.scalar, act_step)

            act_std(2)
            act.wait_ge(s_smallT, 1)
            nc.scalar.activation(wrT[:, :], bank[0][:, 0:E], ACT.Copy).then_inc(s_smallT, 1)
            nc.scalar.activation(b1T[:, :], bank[0][:, E:E + E * FC], ACT.Copy).then_inc(s_smallT, 1)
            act.wait_ge(s_w2T, 1)
            nc.scalar.activation(w2T[:, :, :].rearrange("p a c -> p (a c)"), bank[1][:, :], ACT.Copy).then_inc(s_w2Tc, 1)
            act.wait_ge(s_w2, 16 * (7 + 2 * HS))
            nc.scalar.activation(nlw[:, :], dcy[:, :], ACT.Exp).then_inc(s_texp, 1)
            act.wait_ge(s_tdve, 1)
            act.wait_ge(s_tab, 1)
            nc.scalar.activation(apw[:, :], tt[:, :], ACT.Exp, scale=nlw2[:, 0:1])\
                .then_inc(s_texp, 1)
            act.wait_ge(s_m["zero"], 1)

            def act_mix(it, u):
                s, p = 2 * it + u, u % 2
                if exists(s + 1, CH):
                    q = 1 - p
                    wait(act, s_m["fab"], 2 * s)
                    wait(act, s_m["rec"], s)
                    wait(act, s_m["sum"], s + 2)
                    nc.scalar.activation(esum[:, q, :], bank[4][:, :], ACT.Copy).then_inc(s_m["esum"], 1)
                if exists(s + 2, CH):
                    wait(act, s_m["k"], s + 1)
                    wait(act, s_m["xm"], 2 * s + 2)
                    wait(act, s_m["xT"], s + 3)
                    nc.scalar.activation(xT33[:, p, :, 1:N + 1], time(bank[0][:, :]), ACT.Copy).then_inc(s_m["xc"], 1)
                if exists(s + 1, CH):
                    wait(act, s_m["er1"], s)
                    wait(act, s_m["r"], s + 2)
                    nc.scalar.activation(er[:, q, :], bank[3][:, :], ACT.Exp, scale=-1.0).then_inc(s_m["er"], 1)
                if exists(s + 2, CH):
                    wait(act, s_m["xm"], 2 * s + 4)
                    wait(act, s_m["dx"], s + 3)
                    for k in range(2):
                        last = nc.scalar.activation(mdx[:, k, :], dx[:, :], ACT.Copy, scale=mix[:, 1 + k:2 + k])
                    last.then_inc(s_m["mdx"], 1)
                if exists(s + 1, CH):
                    wait(act, s_m["er"], s + 2)
                    nc.scalar.activation(er1[:, q, :], er[:, q, :], ACT.Copy, bias=1.0).then_inc(s_m["er1"], 1)
                if exists(s + 2, CH):
                    wait(act, s_m["ekv"], s + 1)
                    wait(act, s_m["k"], s + 3)
                    nc.scalar.activation(ek[:, p, :], bank[1][:, :], ACT.Exp).then_inc(s_m["ek"], 1)

            over_pairs(act_mix)(act)

            act_std(3)
            for i in range(CH):
                act.wait_ge(s_f["xT"], i + 1)
                wait(act, s_f["rt"], i - 1)
                nc.scalar.activation(x3T[:, i % 2, :], bank[4 * (i % 2)][:, :], ACT.Copy).then_inc(s_f["xc"], 1)
            for k in range(2 * E):
                dst = (W1h, W2h)[k % 2]
                act.wait_ge(s_w3T, k + 1)
                nc.scalar.activation(dst[:, k // 2, :], bank[4 + k % 4][:, :], ACT.Copy).then_inc(s_w3h, 1)
            act.wait_ge(s_te, 1)
            act.wait_ge(s_f["lg"], CH)

            def act_tile(it, u, expert):
                s = UN * it + u
                if exists(s, NT):
                    v = u % 2
                    e = expert(u)
                    wait(act, s_t["hl"], s - 1)
                    wait(act, s_t["h"], s + 1)
                    act.wait_ge(s_smallT, 3)
                    for f in range(FC):
                        last = nc.scalar.activation(hr[:, v, f, :], bank[2 + v][:, f * P:(f + 1) * P], ACT.Relu,
                                                    bias=b1T[:, bass.ds(FC * e + f, 1)])
                    last.then_inc(s_t["hr"], 1)
                if exists(s + 2, NT):
                    wait(act, s_t["h"], s + 1)
                    wait(act, s_t["xT"], s + 3)
                    nc.scalar.activation(xsh[:, u % 2, :], bank[u % 2][:, 0:P], ACT.Copy).then_inc(s_t["xh"], 1)
                if exists(s, NT):
                    wait(act, s_t["y"], s - 3)
                    wait(act, s_t["hr"], s + 1)
                    nc.scalar.activation(hh[:, u % UN, :, :], hr[:, u % 2, :, :], ACT.Copy).then_inc(s_t["hh"], 1)

            over_tiles(act, act_tile)

        @block.tensor
        def _(pe):
            pe.wait_ge(s_const, 2)
            pe.wait_ge(s_w, 16 * 4)
            for k in range(6):
                src, w = ((wq_r, P), (wk_r, CC), (wv_r, CC))[k // 2]
                wait(pe, s_wTc, k - 1)
                for a in range(4):
                    p = 4 * (k % 2) + a
                    last = nc.tensor.transpose(bank[k % 2][:, a * w:(a + 1) * w], src[:, p * P:(p + 1) * P],
                                               identf[0:w, 0:w])
                last.then_inc(s_wT, 1)
            pe.wait_ge(s_wTc, 6)
            for k in range(CH):
                wait(pe, s_abl, k - 1)
                for a in range(4):
                    lo, pair = (k % 2) * D, (k % 4) // 2 * 4 + a
                    if k < 4:
                        last = nc.tensor.matmul(bank[2 + k % 2][:, a * CC:(a + 1) * CC], wqT[lo:lo + D, pair, :],
                                                wkT[lo:lo + D, pair, :], start=True, stop=True)
                    else:
                        last = nc.tensor.matmul(bank[2 + k % 2][0:CC, a * C:(a + 1) * C], wvT[lo:lo + D, pair, :],
                                                wo_r[lo:lo + D, pair, :], start=True, stop=True)
                last.then_inc(s_ab, 1)
                pe.wait_ge(s_xn1, k + 1)
                wait(pe, s_x1l, k - 1)
                pe_norm_T(k % 2, 4 + k % 2, s_x1T)
                if k >= CH - QT:
                    pe.wait_ge(s_abl, 4)
                    c = k - (CH - QT)
                    pe_q(c, c, slice(0, P), QB[c], 1 if c == 3 else 0)
            pe_ctxT(0, 0, 0)
            pe.wait_ge(s_x1l, CH)
            pe.wait_ge(s_abl, 8)
            pe.wait_ge(s_ql, QT)
            pipeline(nc.tensor, pe_step)

            pe.wait_ge(s_res, G)
            pe.wait_ge(s_w2, 16 * (7 + 2 * HS))
            for a in range(4):
                last = nc.tensor.transpose(bank[1][:, a * P:(a + 1) * P], w2r[:, a, :], identf[:, :])
            last.then_inc(s_w2T, 1)
            pe.wait_ge(s_small, 32)
            nc.tensor.transpose(bank[0][:, 0:E], wrr[:, :], identf[0:E, 0:E])
            nc.tensor.transpose(bank[0][:, E:E + E * FC], b1r[:, :], identf[0:E * FC, 0:E * FC]).then_inc(s_smallT, 1)
            pe.wait_ge(s_w2Tc, 1)
            pe.wait_ge(s_smallT, 3)
            pe.wait_ge(s_tab, 5)
            pe.wait_ge(s_m["w"], 2)

            def pe_mix(it, u):
                s, p = 2 * it + u, u % 2
                if exists(s + 2, CH):
                    wait(pe, s_m["xc"], s + 2)
                    wait(pe, s_m["xn"], s + 3)
                    pe_norm_T(p, 0, s_m["xT"])
                if exists(s + 1, CH):
                    for k, (b, done, free) in enumerate(((2, "v", "ekv"), (3, "r", "er"))):
                        wait(pe, s_m[free], s + 1)
                        wait(pe, s_m["xm"], 2 * s + k + 3)
                        nc.tensor.matmul(bank[b][:, :], w2T[:, 1 + k, :], xm[:, 1 - p, k, :], start=True, stop=True)\
                            .then_inc(s_m[done], 1)
                if exists(s + 2, CH):
                    wait(pe, s_m["ek"], s + 2)
                    wait(pe, s_m["xc"], s + 3)
                    nc.tensor.matmul(bank[1][:, :], wka[:, :], xT33[:, p, :, 1:N + 1], start=True, stop=False)
                    nc.tensor.matmul(bank[1][:, :], wkb[:, :], xT33[:, p, :, 0:N], start=False, stop=True)\
                        .then_inc(s_m["k"], 1)
                    wait(pe, s_m["esum"], s + 2)
                    wait(pe, s_m["ek"], s + 3)
                    nc.tensor.matmul(bank[4][:, :], blk[:, :], ek[:, p, :], start=True, stop=True).then_inc(s_m["sum"], 1)
                if exists(s, CH):
                    wait(pe, s_m["res"], s)
                    wait(pe, s_m["o"], s + 1)
                    for t in range(CT):
                        last = nc.tensor.matmul(bank[5][:, t * P:(t + 1) * P], oT[:, t * P:(t + 1) * P], w2T[:, 3, :],
                                                start=True, stop=True)
                    last.then_inc(s_m["y"], 1)

            over_pairs(pe_mix)(pe)

            for i in range(CH + 1):
                if i < CH:
                    pe.wait_ge(s_f["xn"], i + 1)
                    wait(pe, s_f["xc"], i - 1)
                    pe_norm_T(i % 2, 4 * (i % 2), s_f["xT"])
                if i:
                    k = i - 1
                    pe.wait_ge(s_f["xc"], k + 1)
                    wait(pe, s_f["lg"], k - 1)
                    for t in range(CT):
                        last = nc.tensor.matmul(bank[1 + 4 * (k % 2)][:, t * E:(t + 1) * E],
                                                x3T[:, k % 2, t * P:(t + 1) * P], wrT[:, :], start=True, stop=True)
                    last.then_inc(s_f["rt"], 1)
            pe.wait_ge(s_hot, 1)
            for k, m in enumerate((tri, onesh)):
                nc.tensor.matmul(bank[2 + k][:, 0:G * E], m[:, :], hot[:, :, :].rearrange("p g e -> p (g e)"),
                                 start=True, stop=True).then_inc(s_cnt, 1)
            pe.wait_ge(s_w3r, 32 * E)
            pe.wait_ge(s_f["lg"], CH)
            for k in range(2 * E):
                wait(pe, s_w3l, k - 3)
                for f in range(FC):
                    src = w1r[:, k // 2, f, :] if k % 2 == 0 else w2fr[:, k // 2, f * P:(f + 1) * P]
                    last = nc.tensor.transpose(bank[4 + k % 4][:, f * P:(f + 1) * P], src, identf[:, :])
                last.then_inc(s_w3T, 1)
            pe.wait_ge(s_te, 1)

            def pe_tile(it, u, expert):
                s = UN * it + u
                v = u % 2
                if exists(s, NT):
                    e = expert(u)
                    wait(pe, s_t["xl"], s + 1)
                    wait(pe, s_t["hr"], s - 1)
                    pe.wait_ge(s_w3l, 2 * E)
                    for f in range(FC):
                        for k, (w, a) in enumerate(((W1h, xsh), (W1h, xsl), (W1l, xsh))):
                            last = nc.tensor.matmul(bank[2 + v][:, f * P:(f + 1) * P],
                                                    w[:, bass.ds(e, 1), f * P:(f + 1) * P].rearrange("p o c -> p (o c)"),
                                                    a[:, v, :], start=(k == 0), stop=(k == 2))
                    last.then_inc(s_t["h"], 1)
                if exists(s + 2, NT):
                    wait(pe, s_t["xn"], s + 3)
                    wait(pe, s_t["xl"], s + 1)
                    nc.tensor.transpose(bank[v][:, 0:P], xsn[:, v, :], identf[:, :]).then_inc(s_t["xT"], 1)
                if exists(s - 2, NT):
                    e = expert(u - 2)
                    wait(pe, s_t["hl"], s - 1)
                    wait(pe, s_t["out"], s - 3)
                    pe.wait_ge(s_w3l, 2 * E)
                    for f in range(FC):
                        for k, (a, w) in enumerate(((hh, W2h), (hh, W2l), (hl, W2h))):
                            last = nc.tensor.matmul(bank[4 + v][:, 0:C], a[:, (u - 2) % UN, f, :],
                                                    w[:, bass.ds(e, 1), f * P:(f + 1) * P].rearrange("p o c -> p (o c)"),
                                                    start=(f == 0 and k == 0), stop=(f == FC - 1 and k == 2))
                    last.then_inc(s_t["y"], 1)

            over_tiles(pe, pe_tile)

        @block.vector
        def _(dve):
            chain = Chain(dve, s_ln)
            for k in range(G):
                if k % (G // 4) == 0:
                    dve.wait_ge(s_x[k // (G // 4)], 16)
                dve_stats(k)
            dve_var(chain, 0)
            dve_rstd(chain, 1)
            dve_norm(0, 0, s_xn1)
            for k in range(CH):
                if k + 1 < CH:
                    wait(dve, s_x1T, k)
                    dve_norm(k + 1, (k + 1) % 2, s_xn1)
                dve.wait_ge(s_abh, k + 1)
                if k < 4:
                    nc.vector.scalar_tensor_tensor(heads(Alo, k), bank[2 + k % 2][:, 0:4 * CC].rearrange("p (a c) -> p a c", a=4),
                                                   SCALE, heads(Ahi, k), ALU.mult, ALU.subtract).then_inc(s_abl, 1)
                else:
                    nc.vector.tensor_tensor(heads(Blo, k - 4), bank[2 + k % 2][0:CC, :].rearrange("p (a c) -> p a c", a=4),
                                            heads(Bhi, k - 4), ALU.subtract).then_inc(s_abl, 1)
                dve.wait_ge(s_x1h, k + 1)
                nc.vector.tensor_tensor(x1l[:, T * k:T * (k + 1)], bank[4 + k % 2][:, :], x1h[:, T * k:T * (k + 1)],
                                        ALU.subtract).then_inc(s_x1l, 1)
                if k >= CH - QT:
                    c = k - (CH - QT)
                    dve_q(c, 0, c, QB[c])
            dve_cT(0, 0)
            dve.wait_ge(s_bo, 16 + CH)
            pipeline(nc.vector, dve_step)

            dve.wait_ge(s_res, G)
            dve_stats(G - 1)
            dve_var(chain, LS)
            dve_rstd(chain, 2)
            dve.wait_ge(s_w2, 16 * (7 + 2 * HS))
            chain.link(nc.vector.tensor_scalar(omm[:, :], mix[:, 0:1], -1.0, 1.0, ALU.mult, ALU.add))
            dve.wait_ge(s_texp, 1)
            nc.vector.tensor_scalar(nlw2[:, :], nlw[:, :], -1.0, None, ALU.mult).then_inc(s_tdve, 1)
            dve.wait_ge(s_texp, 2)
            chain.link(nc.vector.reciprocal(iap[:, :], apw[:, :]))
            dve.wait_ge(s_w2Tc, 1)
            nc.vector.tensor_scalar(wka[:, :], w2T[:, 0, :], mix[:, 0:1], None, ALU.mult).then_inc(s_m["w"], 1)
            nc.vector.tensor_scalar(wkb[:, :], w2T[:, 0, :], omm[:, :], None, ALU.mult).then_inc(s_m["w"], 1)
            dve.wait_ge(s_m["zero"], 3)

            def dve_mix(it, u):
                s, p = 2 * it + u, u % 2
                if exists(s - 2, CH):
                    wait(dve, s_m["res"], s - 1)
                if exists(s + 2, CH):
                    wait(dve, s_m["xT"], s + 1)
                    dve_norm(s + 2, p, s_m["xn"])
                if exists(s - 2, CH):
                    for t in range(CT):
                        dve_stats(CT * (s - 2) + t)
                if exists(s - 1, CH):
                    wait(dve, s_m["y"], s)
                    xc = X[:, bass.ds(CT * (s - 1), CT), :]
                    nc.vector.tensor_tensor(xc, xc, bank[5][:, :].rearrange("p (t c) -> p t c", t=CT), ALU.add)\
                        .then_inc(s_m["res"], 1)
                if exists(s, CH):
                    ch = lambda n: wait(dve, s_m["ch"], 7 * s + n)
                    for k in range(2):
                        wait(dve, s_m["st"], 2 * s + k + 1)
                        nc.vector.tensor_scalar(scl[:, k, :], sraw[:, k, :], -FMAX, FMAX, ALU.max, ALU.min)\
                            .then_inc(s_m["ch"], 1)
                    for k in range(2):
                        ch(1 + k)
                        nc.vector.scalar_tensor_tensor(sst[:, k, :], sraw[:, k, :], FMAX, scl[:, k, :],
                                                       ALU.is_le, ALU.mult).then_inc(s_m["ch"], 1)
                if exists(s + 1, CH):
                    q = 1 - p
                    wait(dve, s_m["o"], s)
                    wait(dve, s_m["ek"], s + 2)
                    wait(dve, s_m["v"], s + 2)
                    nc.vector.tensor_tensor(ekv[:, q, :], ek[:, q, :], bank[2][:, :], ALU.mult).then_inc(s_m["ekv"], 1)
                if exists(s, CH):
                    ch(4)
                    nc.vector.scalar_tensor_tensor(den[:, :], esum[:, p, :], nlw[:, 1:2], sst[:, 1, :], ALU.mult, ALU.add)\
                        .then_inc(s_m["ch"], 1)
                    nc.vector.scalar_tensor_tensor(num[:, p, :], ekv[:, p, :], nlw[:, 1:2], sst[:, 0, :], ALU.mult, ALU.add)\
                        .then_inc(s_m["ch"], 1)
                    wait(dve, s_m["er1"], s + 1)
                    ch(5)
                    nc.vector.scalar_tensor_tensor(den[:, :], den[:, :], 1e-6, er1[:, p, :], ALU.max, ALU.mult)\
                        .then_inc(s_m["ch"], 1)
                    ch(7)
                    nc.vector.reciprocal(rec[:, p, :], den[:, :]).then_inc(s_m["rec"], 1)
                if exists(s + 1, CH):
                    for k in range(2):
                        wait(dve, s_m["st"], 2 * s + k + 1)
                        wait(dve, s_m["fab"], 2 * s + k + 3)
                        for b in range(SEQ):
                            last = nc.vector.tensor_tensor_scan(cs[:, k, b, 1:N + 1], onesn[:, :],
                                                                fab[:, k, b * N:(b + 1) * N], 0.0, ALU.mult, ALU.add)
                        last.then_inc(s_m["cs"], 1)

            over_pairs(dve_mix)(dve)

            dve.wait_ge(s_m["res"], CH)
            dve_var(chain, 2 * LS + 2)
            dve_rstd(chain, 3)
            nc.vector.tensor_copy(R[:, :, C + 1], mean[:, :]).then_inc(s_row, 1)
            nc.vector.tensor_copy(R[:, :, C + 2], rst[:, :]).then_inc(s_row, 1)
            dve.wait_ge(s_w3, 32)
            for i in range(-2, CH):
                if i + 2 < CH:
                    wait(dve, s_f["xT"], i + 1)
                    dve_norm(i + 2, i % 2, s_f["xn"])
                if i < 0:
                    continue
                dve.wait_ge(s_f["rt"], i + 1)
                nc.vector.tensor_tensor(lg[:, CT * i:CT * (i + 1), :],
                                        bank[1 + 4 * (i % 2)][:, 0:CT * E].rearrange("p (t e) -> p t e", e=E),
                                        brb[:, :].unsqueeze(1).broadcast_to([P, CT, E]), ALU.add)\
                    .then_inc(s_f["lg"], 1)
            dve.wait_ge(s_f["lg"], CH)
            r = Chain(dve, s_route)
            r.link(nc.vector.tensor_reduce(mx[:, :], lg[:, :, :], AX.X, ALU.max))
            r.link(nc.vector.tensor_tensor(eq[:, :, :], lg[:, :, :], mx[:, :].unsqueeze(2).broadcast_to([P, G, E]),
                                           ALU.is_equal))
            r.link(nc.vector.tensor_tensor(wt[:, :, :], eq[:, :, :], desc[:, :].unsqueeze(1).broadcast_to([P, G, E]),
                                           ALU.mult))
            r.link(nc.vector.tensor_reduce(mx[:, :], wt[:, :, :], AX.X, ALU.max))
            nc.vector.tensor_tensor(hot[:, :, :], wt[:, :, :], mx[:, :].unsqueeze(2).broadcast_to([P, G, E]),
                                    ALU.is_equal).then_inc(s_hot, 1)
            dve.wait_ge(s_cnt, 2)
            r.link(nc.vector.tensor_copy(cnt[:, :, :].rearrange("p g e -> p (g e)"), bank[3][:, 0:G * E]))
            for e in range(E):
                r.mark(nc.vector.tensor_tensor_scan(run[:, :, e], onesr[:, :], cnt[:, :, e], 0.0, ALU.mult, ALU.add))
            dve.wait_ge(s_route, r.count)
            r.mark(nc.vector.tensor_tensor(before[:, :, :], run[:, :, :], cnt[:, :, :], ALU.subtract))
            r.link(nc.vector.tensor_tensor(gt[:, :, :], run[:, G - 1, :].unsqueeze(2).broadcast_to([P, E, G]), kk[:, :, :],
                                           ALU.is_gt))
            r.link(nc.vector.tensor_reduce(tiles[:, :], gt[:, :, :], AX.X, ALU.add))
            r.link(nc.vector.tensor_tensor_scan(ends[:, :], onesr[:, 0:E], tiles[:, :], 0.0, ALU.mult, ALU.add))
            r.mark(nc.vector.tensor_tensor(ge[:, :, :], ti[:, :, :], ends[:, :].unsqueeze(1).broadcast_to([P, NT, E]),
                                           ALU.is_ge))
            r.link(nc.vector.tensor_tensor(offs[:, :], ends[:, :], tiles[:, :], ALU.subtract))
            r.link(nc.vector.scalar_tensor_tensor(before[:, :, :], offs[:, :].unsqueeze(1).broadcast_to([P, G, E]), float(P),
                                                  before[:, :, :], ALU.mult, ALU.add))
            r.link(nc.vector.tensor_tensor(slot[:, :, :], bank[2][:, 0:G * E].rearrange("p (g e) -> p g e", e=E),
                                           before[:, :, :], ALU.add))
            r.link(nc.vector.tensor_tensor(slot[:, :, :], slot[:, :, :], hot[:, :, :], ALU.mult))
            r.link(nc.vector.tensor_reduce(posf[:, :], slot[:, :, :], AX.X, ALU.add))
            nc.vector.tensor_copy(pos[:, :], posf[:, :]).then_inc(s_pos, 1)
            r.link(nc.vector.tensor_reduce(te[:, :], ge[:, :, :], AX.X, ALU.add))
            r.link(nc.vector.memset(tep[:, :], 0.0))
            r.link(nc.vector.tensor_scalar(tep[:, 5:5 + NT], te[:, :], float(E - 1), None, ALU.min))
            digit = lambda k: tep[:, k:k + UN * NK:UN]
            r.link(nc.vector.tensor_copy(pkf[:, :], digit(NV - 1)))
            for k in range(NV - 2, -1, -1):
                r.link(nc.vector.scalar_tensor_tensor(pkf[:, :], pkf[:, :], float(E), digit(k), ALU.mult, ALU.add))
            nc.vector.tensor_copy(pk[:, :], pkf[:, :]).then_inc(s_te, 1)
            for k in range(2 * E):
                hi, lo = ((W1h, W1l), (W2h, W2l))[k % 2]
                dve.wait_ge(s_w3h, k + 1)
                nc.vector.tensor_tensor(lo[:, k // 2, :], bank[4 + k % 4][:, :], hi[:, k // 2, :], ALU.subtract)\
                    .then_inc(s_w3l, 1)
            dve.wait_ge(s_te, 1)

            def dve_tile(it, u, expert):
                s = UN * it + u
                if exists(s + 2, NT):
                    v = u % 2
                    wait(dve, s_t["h"], s + 1)
                    wait(dve, s_t["xh"], s + 3)
                    nc.vector.tensor_tensor(xsl[:, v, :], bank[v][:, 0:P], xsh[:, v, :], ALU.subtract)\
                        .then_inc(s_t["xl"], 1)
                if exists(s + 3, NT):
                    v, w = (u + 1) % 2, (u + 3) % UN
                    wait(dve, s_xs[w], 16 * (it + 1 + (u + 3) // UN))
                    wait(dve, s_t["xT"], s + 2)
                    nc.vector.tensor_scalar(xsn[:, v, :], xs[:, w, 0:C], xs[:, w, C + 1:C + 2], xs[:, w, C + 2:C + 3],
                                            ALU.subtract, ALU.mult).then_inc(s_t["xn"], 1)
                if exists(s, NT):
                    wait(dve, s_t["y"], s - 3)
                    wait(dve, s_t["hh"], s + 1)
                    nc.vector.tensor_tensor(hl[:, u % UN, :, :], hr[:, u % 2, :, :], hh[:, u % UN, :, :], ALU.subtract)\
                        .then_inc(s_t["hl"], 1)
                if exists(s - 2, NT):
                    v, w = u % 2, (u - 2) % UN
                    wait(dve, s_t["yb"], s - 1)
                    wait(dve, s_store[w], 16 * (it + (u - 2) // UN))
                    nc.vector.tensor_copy(idx[:, w:w + 1], yb[:, w, C:C + 1])
                    wait(dve, s_t["y"], s - 1)
                    nc.vector.tensor_tensor(yout[:, w, :], bank[4 + v][:, 0:C], yb[:, w, 0:C], ALU.add)\
                        .then_inc(s_t["out"], 1)

            over_tiles(dve, dve_tile, routed=False)


_INS = ['x', 'ctx_768', 'L0_xattn_Wq', 'L0_xattn_Wk', 'L0_xattn_Wv', 'L0_xattn_Wo', 'L0_xattn_bo',
        'L0_attn_mix_k', 'L0_attn_mix_v', 'L0_attn_mix_r', 'L0_attn_W_key', 'L0_attn_W_value',
        'L0_attn_W_receptance', 'L0_attn_W_output', 'L0_attn_time_decay', 'L0_attn_time_first',
        'L0_ffn_Wr', 'L0_ffn_br', 'L0_ffn_W1', 'L0_ffn_b1', 'L0_ffn_W2', 'L0_ffn_b2']
_OUTS = [((128, 32, 128), 'float32')]


def kernel(**inputs):
    import numpy as _np
    import concourse.bacc as _bacc
    from concourse import mybir as _mybir
    from concourse.bass_utils import run_bass_kernel_spmd as _run

    nc = _bacc.Bacc("TRN2", target_bir_lowering=False, num_devices=1)
    arrays, args = {}, []
    for name in _INS:
        a = _np.ascontiguousarray(inputs[name])
        arrays[f"in_{name}_dram"] = a
        args.append(nc.dram_tensor(f"in_{name}_dram", a.shape, _mybir.dt.from_np(a.dtype), kind="ExternalInput").ap())
    for i, (shape, dtype) in enumerate(_OUTS):
        dt = _mybir.dt.from_np(_np.dtype(dtype))
        args.append(nc.dram_tensor(f"out_{i}_dram", shape, dt, kind="ExternalOutput").ap())
    perceiver_layer_kernel(nc, *args)
    r = _run(nc, [arrays], core_ids=[0])
    return r.results[0]["out_0_dram"]
```
